# Optimizing a Trainium2 kernel written in Bass

```python
import numpy as np
import jax
import jax.numpy as jnp

def _softmax(x, axis=-1):
    return jax.nn.softmax(x, axis=axis)

def _gelu(x):
    return jax.nn.gelu(x, approximate=True)

def _silu(x):
    return jax.nn.silu(x)

def _sigmoid(x):
    return jax.nn.sigmoid(x)

def _layernorm(x, axis=-1, eps=1e-05):
    m = jnp.mean(x, axis=axis, keepdims=True)
    v = jnp.var(x, axis=axis, keepdims=True)
    return (x - m) / jnp.sqrt(v + eps)

def _scatter_add(tgt, idx, src, axis=0):
    return tgt.at[idx].add(src)

def _segment_sum(src, seg, n):
    return jax.ops.segment_sum(src, seg, n)
kernel_name = 'mk_vit_tower_cls_d2_tok_img768_r4_0fd8e4'

def setup_inputs(seed: int=0):
    np.random.seed(seed)
    _w = jnp.asarray

    def _rec_inputs():
        import jax
        import jax.numpy as jnp
        _rk = jax.random.key(seed)
        x = -0.000356955 + 1 * jax.random.normal(jax.random.fold_in(_rk, 1), (128, 3, 64, 64), jnp.float32)
        cls_tok = 0.02 * jax.random.normal(jax.random.fold_in(_rk, 5), (1, 1, 192), jnp.float32)
        return (x, cls_tok)
    x, cls_tok = _rec_inputs()

    def _L0_tok_setup():
        import jax, jax.numpy as jnp
        import numpy as np
        PATCH = 16
        C = 3
        EMBED = 192

        def _patchify(x, p):
            B, Cc, H, W = x.shape
            gh, gw = (H // p, W // p)
            x = x.reshape(B, Cc, gh, p, gw, p)
            x = x.transpose(0, 2, 4, 1, 3, 5)
            return x.reshape(B, gh * gw, Cc * p * p)
        key = jax.random.key(seed)
        k1, k2, k3 = jax.random.split(key, 3)
        x = jax.random.normal(k1, (128, C, 224, 224), dtype=jnp.float32)
        fan_in = PATCH * PATCH * C
        bound = 1.0 / np.sqrt(fan_in)
        W = jax.random.uniform(k2, (EMBED, fan_in), dtype=jnp.float32, minval=-bound, maxval=bound)
        b = jax.random.uniform(k3, (EMBED,), dtype=jnp.float32, minval=-bound, maxval=bound)
        return {'x': x, 'W': W, 'b': b}
    _L0_tok_all = _L0_tok_setup()
    _L0_tok_in = {k: v for k, v in _L0_tok_all.items() if k in ('W', 'b')}
    del _L0_tok_all

    def _L0_attn_setup():
        import jax, jax.numpy as jnp
        import numpy as np
        B, N, DIM = (16, 577, 192)
        HEADS, DIM_HEAD = (12, 64)
        INNER = HEADS * DIM_HEAD
        key = jax.random.key(seed)
        k1, k2, k3, k4 = jax.random.split(key, 4)
        x = jax.random.normal(k1, (B, N, DIM), dtype=jnp.float32)
        w_qkv = jax.random.normal(k2, (DIM, 3 * INNER), dtype=jnp.float32) * 0.02
        scale = jnp.full((HEADS,), DIM_HEAD ** (-0.5), dtype=jnp.float32)
        w_out = jax.random.normal(k3, (INNER, DIM), dtype=jnp.float32) * 0.02
        b_out = jnp.zeros((DIM,), dtype=jnp.float32)
        return {'x': x, 'w_qkv': w_qkv, 'scale': scale, 'w_out': w_out, 'b_out': b_out}
    _L0_attn_all = _L0_attn_setup()
    _L0_attn_in = {k: v for k, v in _L0_attn_all.items() if k in ('w_qkv', 'scale', 'w_out', 'b_out')}
    del _L0_attn_all

    def _L0_ffn_setup():
        import jax, jax.numpy as jnp
        import numpy as np
        EPS_NORM = 1e-06
        EPS_Q = 1e-05

        def rmsnorm(x, g):
            return x * jax.lax.rsqrt(jnp.mean(x * x, axis=-1, keepdims=True) + EPS_NORM) * g

        def activation_quant(x):
            scale = 127.0 / jnp.maximum(jnp.max(jnp.abs(x), axis=-1, keepdims=True), EPS_Q)
            return jnp.clip(jnp.round(x * scale), -128, 127) / scale

        def weight_quant(w):
            scale = 1.0 / jnp.maximum(jnp.mean(jnp.abs(w)), EPS_Q)
            return jnp.clip(jnp.round(w * scale), -1, 1) / scale

        def bitlinear(x, w, g):
            x_norm = rmsnorm(x, g)
            x_q = x_norm + jax.lax.stop_gradient(activation_quant(x_norm) - x_norm)
            w_q = w + jax.lax.stop_gradient(weight_quant(w) - w)
            return jnp.einsum('bsd,od->bso', x_q, w_q)
        key = jax.random.key(seed)
        k1, k2, k3 = jax.random.split(key, 3)
        B, S, D, H = (8, 1024, 192, 512)
        x = jax.random.normal(k1, (B, S, D), dtype=jnp.float32)
        w_in = jax.random.normal(k2, (2 * H, D), dtype=jnp.float32) * 0.002
        w_out = jax.random.normal(k3, (D, H), dtype=jnp.float32) * 0.002
        g_in = jnp.ones((D,), dtype=jnp.float32)
        g_out = jnp.ones((H,), dtype=jnp.float32)
        return {'x': x, 'w_in': w_in, 'g_in': g_in, 'w_out': w_out, 'g_out': g_out}
    _L0_ffn_all = _L0_ffn_setup()
    _L0_ffn_in = {k: v for k, v in _L0_ffn_all.items() if k in ('w_in', 'g_in', 'w_out', 'g_out')}
    del _L0_ffn_all

    def _L1_attn_setup():
        import jax, jax.numpy as jnp
        import numpy as np
        import math
        H = 12

        def _ln(x, w, b, eps=1e-05):
            mu = x.mean(-1, keepdims=True)
            var = ((x - mu) ** 2).mean(-1, keepdims=True)
            return (x - mu) / jnp.sqrt(var + eps) * w + b

        def _reference_tuple_inner(x, Wqkv, bqkv, Wb1, Wb2, temperature, Wproj, bproj, ln_w, ln_b, mn_w, mn_b):
            B, L, D = x.shape
            d = D // H
            x_norm = _ln(x, ln_w, ln_b)
            qkv = x_norm @ Wqkv + bqkv
            q, k, v = jnp.split(qkv, 3, axis=-1)
            params = (jax.nn.silu(x @ Wb1) @ Wb2).reshape(B, L, H, 5)
            sem_amp = jax.nn.sigmoid(params[..., 0])
            sem_phase = jnp.tanh(params[..., 1]) * math.pi
            ctx_amp = jax.nn.sigmoid(params[..., 2])
            ctx_phase = jnp.tanh(params[..., 3]) * math.pi
            temp = jnp.clip(temperature, 0.1, 2.0)
            interference = jnp.tanh(sem_amp * ctx_amp * jnp.cos(sem_phase - ctx_phase)) * temp
            gate = jax.nn.sigmoid(interference)
            q_f = (jax.nn.elu(q) + 1.0).reshape(B, L, H, d)
            k_f = (jax.nn.elu(k) + 1.0).reshape(B, L, H, d)
            v_f = v.reshape(B, L, H, d)
            kv_gated = jnp.einsum('blhd,blhe->blhde', k_f, v_f) * (1.0 + gate)[..., None, None]
            kv_states = jnp.cumsum(kv_gated, axis=1)
            z_states = jnp.cumsum(k_f, axis=1)
            out_num = jnp.einsum('blhd,blhde->blhe', q_f, kv_states)
            den = jnp.sum(q_f * z_states, axis=-1, keepdims=True) + 1e-06
            out = _ln(out_num / den, mn_w, mn_b)
            attn_out = out.reshape(B, L, D)
            return (attn_out @ Wproj + bproj, gate)
        key = jax.random.key(seed)
        B, L, D, R = (2, 256, 192, 128)
        d_head = D // H
        ks = jax.random.split(key, 6)
        s = 0.02
        return {'x': jax.random.normal(ks[0], (B, L, D), jnp.float32), 'Wqkv': jax.random.normal(ks[1], (D, 3 * D), jnp.float32) * s, 'bqkv': jnp.zeros((3 * D,), jnp.float32), 'Wb1': jax.random.normal(ks[2], (D, R), jnp.float32) * s, 'Wb2': jax.random.normal(ks[3], (R, H * 5), jnp.float32) * s, 'temperature': jnp.ones((1,), jnp.float32) * 0.5, 'Wproj': jax.random.normal(ks[4], (D, D), jnp.float32) * s, 'bproj': jnp.zeros((D,), jnp.float32), 'ln_w': jnp.ones((D,), jnp.float32), 'ln_b': jnp.zeros((D,), jnp.float32), 'mn_w': jnp.ones((d_head,), jnp.float32), 'mn_b': jnp.zeros((d_head,), jnp.float32)}
    _L1_attn_all = _L1_attn_setup()
    _L1_attn_in = {k: v for k, v in _L1_attn_all.items() if k in ('Wqkv', 'bqkv', 'Wb1', 'Wb2', 'temperature', 'Wproj', 'bproj', 'ln_w', 'ln_b', 'mn_w', 'mn_b')}
    del _L1_attn_all

    def _L1_ffn_setup():
        import jax, jax.numpy as jnp
        import numpy as np
        HIDDEN = 192
        INNER = 128
        EPS = 1e-05
        key = jax.random.key(seed)
        ks = jax.random.split(key, 6)
        B, S = (8, 1024)
        x = jax.random.normal(ks[0], (B, S, HIDDEN), dtype=jnp.float32)
        W1 = jax.random.normal(ks[1], (INNER, HIDDEN), dtype=jnp.float32) * 0.02
        b1 = jnp.zeros((INNER,), dtype=jnp.float32)
        W2 = jax.random.normal(ks[2], (HIDDEN, INNER), dtype=jnp.float32) * 0.02
        b2 = jnp.zeros((HIDDEN,), dtype=jnp.float32)
        bound = 1.0 / np.sqrt(HIDDEN)
        Wo = jax.random.uniform(ks[3], (HIDDEN, HIDDEN), minval=-bound, maxval=bound, dtype=jnp.float32)
        bo = jax.random.uniform(ks[4], (HIDDEN,), minval=-bound, maxval=bound, dtype=jnp.float32)
        gamma = jnp.ones((HIDDEN,), dtype=jnp.float32)
        beta = jnp.zeros((HIDDEN,), dtype=jnp.float32)
        return {'x': x, 'W1': W1, 'b1': b1, 'W2': W2, 'b2': b2, 'Wo': Wo, 'bo': bo, 'gamma': gamma, 'beta': beta}
    _L1_ffn_all = _L1_ffn_setup()
    _L1_ffn_in = {k: v for k, v in _L1_ffn_all.items() if k in ('W1', 'b1', 'W2', 'b2', 'Wo', 'bo', 'gamma', 'beta')}
    del _L1_ffn_all
    return {'x': x, 'cls_tok': cls_tok, 'L0_tok_W': _L0_tok_in['W'], 'L0_tok_b': _L0_tok_in['b'], 'L0_attn_w_qkv': _L0_attn_in['w_qkv'], 'L0_attn_scale': _L0_attn_in['scale'], 'L0_attn_w_out': _L0_attn_in['w_out'], 'L0_attn_b_out': _L0_attn_in['b_out'], 'L0_ffn_w_in': _L0_ffn_in['w_in'], 'L0_ffn_g_in': _L0_ffn_in['g_in'], 'L0_ffn_w_out': _L0_ffn_in['w_out'], 'L0_ffn_g_out': _L0_ffn_in['g_out'], 'L1_attn_Wqkv': _L1_attn_in['Wqkv'], 'L1_attn_bqkv': _L1_attn_in['bqkv'], 'L1_attn_Wb1': _L1_attn_in['Wb1'], 'L1_attn_Wb2': _L1_attn_in['Wb2'], 'L1_attn_temperature': _L1_attn_in['temperature'], 'L1_attn_Wproj': _L1_attn_in['Wproj'], 'L1_attn_bproj': _L1_attn_in['bproj'], 'L1_attn_ln_w': _L1_attn_in['ln_w'], 'L1_attn_ln_b': _L1_attn_in['ln_b'], 'L1_attn_mn_w': _L1_attn_in['mn_w'], 'L1_attn_mn_b': _L1_attn_in['mn_b'], 'L1_ffn_W1': _L1_ffn_in['W1'], 'L1_ffn_b1': _L1_ffn_in['b1'], 'L1_ffn_W2': _L1_ffn_in['W2'], 'L1_ffn_b2': _L1_ffn_in['b2'], 'L1_ffn_Wo': _L1_ffn_in['Wo'], 'L1_ffn_bo': _L1_ffn_in['bo'], 'L1_ffn_gamma': _L1_ffn_in['gamma'], 'L1_ffn_beta': _L1_ffn_in['beta']}

def reference(x, cls_tok, L0_tok_W, L0_tok_b, L0_attn_w_qkv, L0_attn_scale, L0_attn_w_out, L0_attn_b_out, L0_ffn_w_in, L0_ffn_g_in, L0_ffn_w_out, L0_ffn_g_out, L1_attn_Wqkv, L1_attn_bqkv, L1_attn_Wb1, L1_attn_Wb2, L1_attn_temperature, L1_attn_Wproj, L1_attn_bproj, L1_attn_ln_w, L1_attn_ln_b, L1_attn_mn_w, L1_attn_mn_b, L1_ffn_W1, L1_ffn_b1, L1_ffn_W2, L1_ffn_b2, L1_ffn_Wo, L1_ffn_bo, L1_ffn_gamma, L1_ffn_beta):
    import jax
    import jax.numpy as jnp

    def _L0_tok_ref(x, W, b):
        import jax, jax.numpy as jnp
        import numpy as np
        PATCH = 16
        C = 3
        EMBED = 192

        def _patchify(x, p):
            B, Cc, H, W = x.shape
            gh, gw = (H // p, W // p)
            x = x.reshape(B, Cc, gh, p, gw, p)
            x = x.transpose(0, 2, 4, 1, 3, 5)
            return x.reshape(B, gh * gw, Cc * p * p)
        patches = _patchify(x, PATCH)
        return jnp.einsum('blf,ef->ble', patches, W) + b

    def _L0_attn_ref(x, w_qkv, scale, w_out, b_out):
        import jax, jax.numpy as jnp
        import numpy as np
        B, N, DIM = (16, 577, 192)
        HEADS, DIM_HEAD = (12, 64)
        INNER = HEADS * DIM_HEAD
        b, n, _ = x.shape
        h = scale.shape[0]
        dh = w_qkv.shape[1] // (3 * h)
        qkv = x @ w_qkv
        q, k, v = jnp.split(qkv, 3, axis=-1)
        to_heads = lambda t: t.reshape(b, n, h, dh).transpose(0, 2, 1, 3)
        q, k, v = (to_heads(q), to_heads(k), to_heads(v))
        dots = jnp.einsum('bhid,bhjd->bhij', q, k) * scale[None, :, None, None]
        se = dots.mean(axis=1, keepdims=True)
        diag = jnp.eye(n, dtype=bool)
        neg_inf = jnp.array(-jnp.inf, dots.dtype)
        dots = jnp.where(diag, neg_inf, dots)
        top_k = int(n * 0.75)
        _, idx = jax.lax.top_k(dots, top_k)
        bi = jnp.arange(b)[:, None, None, None]
        hi = jnp.arange(h)[None, :, None, None]
        ii = jnp.arange(n)[None, None, :, None]
        keep = jnp.zeros((b, h, n, n), dtype=bool).at[bi, hi, ii, idx].set(True)
        dots = jnp.where(keep, dots, neg_inf) + se
        attn = jax.nn.softmax(dots, axis=-1)
        out = jnp.einsum('bhij,bhjd->bhid', attn, v)
        out = out.transpose(0, 2, 1, 3).reshape(b, n, h * dh)
        return out @ w_out + b_out

    def _L0_ffn_ref(x, w_in, g_in, w_out, g_out):
        import jax, jax.numpy as jnp
        import numpy as np
        EPS_NORM = 1e-06
        EPS_Q = 1e-05

        def rmsnorm(x, g):
            return x * jax.lax.rsqrt(jnp.mean(x * x, axis=-1, keepdims=True) + EPS_NORM) * g

        def activation_quant(x):
            scale = 127.0 / jnp.maximum(jnp.max(jnp.abs(x), axis=-1, keepdims=True), EPS_Q)
            return jnp.clip(jnp.round(x * scale), -128, 127) / scale

        def weight_quant(w):
            scale = 1.0 / jnp.maximum(jnp.mean(jnp.abs(w)), EPS_Q)
            return jnp.clip(jnp.round(w * scale), -1, 1) / scale

        def bitlinear(x, w, g):
            x_norm = rmsnorm(x, g)
            x_q = x_norm + jax.lax.stop_gradient(activation_quant(x_norm) - x_norm)
            w_q = w + jax.lax.stop_gradient(weight_quant(w) - w)
            return jnp.einsum('bsd,od->bso', x_q, w_q)
        h = bitlinear(x, w_in, g_in)
        up, gate = jnp.split(h, 2, axis=-1)
        y = jax.nn.silu(gate) * up
        return bitlinear(y, w_out, g_out)

    def _L1_attn_ref(x, Wqkv, bqkv, Wb1, Wb2, temperature, Wproj, bproj, ln_w, ln_b, mn_w, mn_b):
        import jax, jax.numpy as jnp
        import numpy as np
        import math
        H = 12

        def _ln(x, w, b, eps=1e-05):
            mu = x.mean(-1, keepdims=True)
            var = ((x - mu) ** 2).mean(-1, keepdims=True)
            return (x - mu) / jnp.sqrt(var + eps) * w + b

        def _reference_tuple_inner(x, Wqkv, bqkv, Wb1, Wb2, temperature, Wproj, bproj, ln_w, ln_b, mn_w, mn_b):
            B, L, D = x.shape
            d = D // H
            x_norm = _ln(x, ln_w, ln_b)
            qkv = x_norm @ Wqkv + bqkv
            q, k, v = jnp.split(qkv, 3, axis=-1)
            params = (jax.nn.silu(x @ Wb1) @ Wb2).reshape(B, L, H, 5)
            sem_amp = jax.nn.sigmoid(params[..., 0])
            sem_phase = jnp.tanh(params[..., 1]) * math.pi
            ctx_amp = jax.nn.sigmoid(params[..., 2])
            ctx_phase = jnp.tanh(params[..., 3]) * math.pi
            temp = jnp.clip(temperature, 0.1, 2.0)
            interference = jnp.tanh(sem_amp * ctx_amp * jnp.cos(sem_phase - ctx_phase)) * temp
            gate = jax.nn.sigmoid(interference)
            q_f = (jax.nn.elu(q) + 1.0).reshape(B, L, H, d)
            k_f = (jax.nn.elu(k) + 1.0).reshape(B, L, H, d)
            v_f = v.reshape(B, L, H, d)
            kv_gated = jnp.einsum('blhd,blhe->blhde', k_f, v_f) * (1.0 + gate)[..., None, None]
            kv_states = jnp.cumsum(kv_gated, axis=1)
            z_states = jnp.cumsum(k_f, axis=1)
            out_num = jnp.einsum('blhd,blhde->blhe', q_f, kv_states)
            den = jnp.sum(q_f * z_states, axis=-1, keepdims=True) + 1e-06
            out = _ln(out_num / den, mn_w, mn_b)
            attn_out = out.reshape(B, L, D)
            return (attn_out @ Wproj + bproj, gate)
        return _reference_tuple_inner(x, Wqkv, bqkv, Wb1, Wb2, temperature, Wproj, bproj, ln_w, ln_b, mn_w, mn_b)[0]

    def _L1_ffn_ref(x, W1, b1, W2, b2, Wo, bo, gamma, beta):
        import jax, jax.numpy as jnp
        import numpy as np
        HIDDEN = 192
        INNER = 128
        EPS = 1e-05
        h = jax.nn.relu(jnp.einsum('bsd,id->bsi', x, W1) + b1)
        pred = jnp.einsum('bsi,di->bsd', h, W2) + b2
        out = jnp.einsum('bsd,ed->bse', pred, Wo) + bo
        mu = jnp.mean(out, axis=-1, keepdims=True)
        var = jnp.mean(jnp.square(out - mu), axis=-1, keepdims=True)
        out = (out - mu) * jax.lax.rsqrt(var + EPS) * gamma + beta
        return out
    h = _L0_tok_ref(x, L0_tok_W, L0_tok_b)
    h = jnp.concatenate([jnp.broadcast_to(cls_tok, (h.shape[0], 1, h.shape[2])), h], axis=1)
    h = h + _L0_attn_ref(_layernorm(h, axis=-1), L0_attn_w_qkv, L0_attn_scale, L0_attn_w_out, L0_attn_b_out)
    h = h + _L0_ffn_ref(_layernorm(h, axis=-1), L0_ffn_w_in, L0_ffn_g_in, L0_ffn_w_out, L0_ffn_g_out)
    h = h + _L1_attn_ref(_layernorm(h, axis=-1), L1_attn_Wqkv, L1_attn_bqkv, L1_attn_Wb1, L1_attn_Wb2, L1_attn_temperature, L1_attn_Wproj, L1_attn_bproj, L1_attn_ln_w, L1_attn_ln_b, L1_attn_mn_w, L1_attn_mn_b)
    h = h + _L1_ffn_ref(_layernorm(h, axis=-1), L1_ffn_W1, L1_ffn_b1, L1_ffn_W2, L1_ffn_b2, L1_ffn_Wo, L1_ffn_bo, L1_ffn_gamma, L1_ffn_beta)
    return h

_drawn_inputs = setup_inputs


def setup_inputs(seed=0):
    import zlib

    import numpy as np

    out = dict(_drawn_inputs(seed))
    spreads = {'L0_attn_scale': (0.125, 0.6),
     'L0_attn_b_out': (0.0, 0.1),
     'L0_ffn_g_in': (1.0, 0.6),
     'L0_ffn_g_out': (1.0, 0.6),
     'L1_attn_bqkv': (0.0, 0.1),
     'L1_attn_bproj': (0.0, 0.1),
     'L1_attn_ln_w': (1.0, 0.2),
     'L1_attn_ln_b': (0.0, 0.1),
     'L1_attn_mn_w': (1.0, 0.2),
     'L1_attn_mn_b': (0.0, 0.27),
     'L1_ffn_b1': (0.0, 0.1),
     'L1_ffn_b2': (0.0, 0.1),
     'L1_ffn_gamma': (1.0, 0.2),
     'L1_ffn_beta': (0.0, 0.1)}
    factors = {'L0_ffn_w_in': 7.546, 'L0_ffn_w_out': 8.0, 'L1_attn_Wb1': 8.0, 'L1_attn_Wb2': 8.0}
    for name, (base, spread) in spreads.items():
        noise = np.random.default_rng([zlib.crc32(name.encode()), seed]).standard_normal(out[name].shape)
        drawn = base * np.exp(spread * noise) if base else spread * noise
        out[name] = jnp.asarray(drawn.astype(out[name].dtype))
    for name, factor in factors.items():
        out[name] = (out[name] * factor).astype(out[name].dtype)
    return out
```

```python
from contextlib import ExitStack

import numpy as np

import concourse.bass as bass
from concourse import mybir

F32 = mybir.dt.float32
BF16 = mybir.dt.bfloat16
ALU = mybir.AluOpType
ACT = mybir.ActivationFunctionType
X = mybir.AxisListType.X

IMAGES, CHANNELS, SIDE = 128, 3, 64
PATCH = 16
GRID = SIDE // PATCH
TOKENS = GRID * GRID + 1
EMBED = 192
PER = 7
ROWS = PER * TOKENS
GROUPS = -(-IMAGES // PER)
LAST_IMAGE = IMAGES - PER
STRIPS = PER * CHANNELS * GRID
CHUNKS = CHANNELS * PATCH * PATCH // 128
HALF = EMBED // 2
HEADS = 12
HEAD0 = 64
INNER = HEADS * HEAD0
QTILES = INNER // 128
KEEP = int(TOKENS * 0.75)
DROP = TOKENS - 1 - KEEP
HIDDEN0 = 512
HEAD1 = EMBED // HEADS
HIDDEN1 = 128
GATES = 5
SINE_ORDER = 6
STAGES = 5
STEPS = GROUPS + STAGES - 1

BIG = float(2.0 ** 100)
FILLER = -float(2.0 ** 110)
ROUND = 1.5 * 2.0 ** 23
EPS = 1e-5
EPS_RMS = 1e-6
EPS_QUANT = 1e-5
EPS_DEN = 1e-6

C_IDENT, C_SCORE, C_BLOCK, C_CAUSAL, C_KIND, C_PARITY = 0, 128, 256, 384, 512, 640
C_WIDTH = 642


def constant_table():
    t = np.zeros((128, C_WIDTH), np.float32)
    image = np.arange(ROWS) // TOKENS
    same = image[:, None] == image[None, :]
    t[:, C_IDENT:C_IDENT + 128] = np.eye(128)
    t[:ROWS, C_SCORE:C_SCORE + ROWS] = np.where(same, np.where(np.eye(ROWS, dtype=bool), BIG, 0.0), -BIG)
    t[:ROWS, C_BLOCK:C_BLOCK + ROWS] = same
    t[:ROWS, C_CAUSAL:C_CAUSAL + ROWS] = same & (np.arange(ROWS)[:, None] <= np.arange(ROWS)[None, :])
    t[0, C_KIND:C_KIND + ROWS] = np.arange(ROWS) % TOKENS > 0
    t[1, C_KIND:C_KIND + ROWS] = np.arange(ROWS) % TOKENS == 0
    t[:, C_PARITY] = np.arange(128) % 32 < HEAD1
    t[:, C_PARITY + 1] = np.arange(128) % 32 >= HEAD1
    return t


def sine_coefficients():
    w = np.sqrt((np.cos(np.pi * (np.arange(64) + 0.5) / 64) + 1) / 2)
    c = np.polyfit(w * w, np.sqrt(2) * np.sin(np.pi * w) / (2 * w), SINE_ORDER)
    return [float(x / 4.0 ** (SINE_ORDER - n)) for n, x in enumerate(c)]


def build(nc, a, table, out):
    ctx = ExitStack()
    with ctx:
        def sb(name, shape, dt=F32):
            return ctx.enter_context(nc.sbuf_tensor(name, shape, dt))

        def sem(name):
            return ctx.enter_context(nc.semaphore(name))

        consts = sb("consts", [128, C_WIDTH])
        ident = consts[:, C_IDENT:C_IDENT + 128]
        block_mask = consts[0:ROWS, C_BLOCK:C_BLOCK + ROWS]
        causal_mask = consts[0:ROWS, C_CAUSAL:C_CAUSAL + ROWS]
        token_kind = consts[0:2, C_KIND:C_KIND + ROWS]
        ident_b = sb("ident_b", [128, 128], BF16)
        score_mask_b = sb("score_mask_b", [ROWS, ROWS], BF16)
        ones = sb("ones", [128, 128])
        minus_half = sb("minus_half", [128, HEADS])
        gain_eps = sb("gain_eps", [128, 8])
        eps_head = sb("eps_head", [128, HEADS])
        sine_terms = sb("sine_terms", [128, SINE_ORDER + 1, HEADS])

        w_tok_raw = sb("w_tok_raw", [HALF, 2, CHUNKS * 128])
        w_tok = sb("w_tok", [128, CHUNKS, EMBED])
        start_rows = sb("start_rows", [2, EMBED])
        w_qkv0 = sb("w_qkv0", [HALF, 2, 3 * INNER])
        scale_b = sb("scale_b", [HALF, HEADS])
        w_o0 = sb("w_o0", [128, QTILES, EMBED])
        b_o0 = sb("b_o0", [1, EMBED])
        w_in_raw = sb("w_in_raw", [128, 2 * HIDDEN0 // 128, EMBED])
        w_in_q = sb("w_in_q", [128, 2 * HIDDEN0 // 128, EMBED], BF16)
        w_in = sb("w_in", [HALF, 2, 2 * HIDDEN0], BF16)
        g_in = sb("g_in", [ROWS, EMBED])
        w_out_raw = sb("w_out_raw", [HALF, 2, HIDDEN0])
        w_out_q = sb("w_out_q", [HALF, 2, HIDDEN0], BF16)
        w_out = sb("w_out", [128, HIDDEN0 // 128, EMBED], BF16)
        g_out = sb("g_out", [ROWS, HIDDEN0])
        abs_sums = sb("abs_sums", [128, 2])
        w_scale = sb("w_scale", [128, 2])
        w_scale_inv = sb("w_scale_inv", [128, 2])
        w_scale_127 = sb("w_scale_127", [128, 2])
        w_qkv1 = sb("w_qkv1", [HALF + 1, 2, 3 * EMBED])
        w_qkv1_raw = sb("w_qkv1_raw", [HALF, 2, 3 * EMBED])
        ln_wb = sb("ln_wb", [HALF, 2, 2])
        b_qkv1 = sb("b_qkv1", [1, 3 * EMBED])
        w_g1 = sb("w_g1", [HALF, 2, HIDDEN1])
        w_g2 = sb("w_g2", [HIDDEN1, HEADS, GATES])
        temp = sb("temp", [ROWS, 1])
        w_p1_raw = sb("w_p1_raw", [HALF, 2, EMBED])
        w_p1 = sb("w_p1", [HALF + 1, 2, EMBED])
        b_p1 = sb("b_p1", [1, EMBED])
        mn_wb = sb("mn_wb", [HALF, 2])
        w1_raw = sb("w1_raw", [HIDDEN1, EMBED])
        w1 = sb("w1", [HALF + 1, 2, HIDDEN1])
        w2_raw = sb("w2_raw", [HALF, 2, HIDDEN1])
        wo_raw = sb("wo_raw", [HALF, 2, EMBED])
        wo = sb("wo", [HALF, 2, EMBED])
        b2_col = sb("b2_col", [HALF, 2])
        w2o = sb("w2o", [HIDDEN1, EMBED])
        b2o = sb("b2o", [1, EMBED])
        bo = sb("bo", [1, EMBED])
        gamma = sb("gamma", [ROWS, EMBED])
        beta = sb("beta", [ROWS, EMBED])

        strips = sb("strips", [STRIPS, 2, PATCH, SIDE])
        patches = sb("patches", [STRIPS, GRID, PATCH * PATCH])
        patchT = sb("patchT", [128, CHUNKS, ROWS])
        h0 = sb("h0", [ROWS, 2, EMBED])
        stats0 = sb("stats0", [ROWS, 6])
        moments0 = sb("moments0", [ROWS, 2])
        spread0 = sb("spread0", [ROWS, 1])
        rstd0 = sb("rstd0", [ROWS, 1])
        norm0 = sb("norm0", [ROWS, EMBED])
        norm0T = sb("norm0T", [HALF, 2, ROWS])
        qkT = sb("qkT", [128, 2, 2 * QTILES, ROWS])
        v0 = sb("v0", [ROWS, 2, INNER])

        ROWLEN = TOKENS + 8 - DROP - 1
        scores = sb("scores", [ROWS, HEADS, ROWLEN])
        score_sum = sb("score_sum", [ROWS, TOKENS])
        top = sb("top", [ROWS, HEADS, 8])
        kept = sb("kept", [ROWS, HEADS, ROWLEN])
        mixed = sb("mixed", [ROWS, HEADS, TOKENS])
        least = sb("least", [ROWS, HEADS])
        shifted = sb("shifted", [ROWS, HEADS, TOKENS])
        expd = sb("expd", [ROWS, HEADS, TOKENS])
        exp_sum = sb("exp_sum", [ROWS, HEADS])
        exp_inv = sb("exp_inv", [ROWS, HEADS])
        probs = sb("probs", [ROWS, HEADS, TOKENS])
        wide = sb("wide", [ROWS, HEADS, PER, TOKENS])
        probsT = sb("probsT", [ROWS, HEADS, ROWS])
        att0T = sb("att0T", [128, QTILES, ROWS])
        h1 = sb("h1", [ROWS, 2, EMBED])

        stats1 = sb("stats1", [ROWS, 6])
        moments1 = sb("moments1", [ROWS, 2])
        spread1 = sb("spread1", [ROWS, 2])
        rstd1 = sb("rstd1", [ROWS, 1])
        u_in = sb("u_in", [ROWS, EMBED])
        umax_in = sb("umax_in", [ROWS, 1])
        amax_in = sb("amax_in", [ROWS, 1])
        ainv_in = sb("ainv_in", [ROWS, 1])
        quant_in = sb("quant_in", [ROWS, 1])
        unit_in = sb("unit_in", [ROWS, 2])
        big_in = sb("big_in", [ROWS, EMBED])
        int_in = sb("int_in", [ROWS, EMBED], BF16)
        int_inT = sb("int_inT", [HALF, 2, ROWS], BF16)
        tanh_gate = sb("tanh_gate", [ROWS, HIDDEN0])
        gated = sb("gated", [ROWS, HIDDEN0])
        product = sb("product", [ROWS, HIDDEN0])
        scaled = sb("scaled", [ROWS, HIDDEN0])
        squares = sb("squares", [ROWS, HIDDEN0])
        half_c2 = sb("half_c2", [ROWS, 2])
        square_sum = sb("square_sum", [ROWS, 1])
        mean_square = sb("mean_square", [ROWS, 1])
        rms_inv = sb("rms_inv", [ROWS, 1])
        row_gain = sb("row_gain", [ROWS, 1])
        umax_out = sb("umax_out", [ROWS, 1])
        amax_out = sb("amax_out", [ROWS, 1])
        ainv_out = sb("ainv_out", [ROWS, 1])
        quant_out = sb("quant_out", [ROWS, 1])
        unit_out = sb("unit_out", [ROWS, 1])
        big_out = sb("big_out", [ROWS, HIDDEN0])
        int_out = sb("int_out", [ROWS, HIDDEN0], BF16)
        int_outT = sb("int_outT", [128, HIDDEN0 // 128, ROWS], BF16)
        h2 = sb("h2", [ROWS, 2, EMBED])

        stats2 = sb("stats2", [ROWS, 6])
        moments2 = sb("moments2", [ROWS, 2])
        spread2 = sb("spread2", [ROWS, 2, 2])
        rstd2 = sb("rstd2", [ROWS, 2])
        norms2 = sb("norms2", [ROWS, 2, EMBED])
        norms2T = sb("norms2T", [HALF + 1, 4, ROWS])
        exp_qk = sb("exp_qk", [HALF, 4, ROWS])
        relu_qk = sb("relu_qk", [HALF, 4, ROWS])
        feat_qk = sb("feat_qk", [HALF, 4, ROWS])
        feat_k = sb("feat_k", [HALF, 2, 2, ROWS])
        tanh_hid = sb("tanh_hid", [HIDDEN1, ROWS])
        hidT = sb("hidT", [HIDDEN1, ROWS])
        tanh_par = sb("tanh_par", [ROWS, HEADS, GATES])
        wave = sb("wave", [ROWS, HEADS])
        wave_sq = sb("wave_sq", [ROWS, HEADS])
        poly = sb("poly", [ROWS, 2, HEADS])
        amp = sb("amp", [ROWS, 2, HEADS])
        amps = sb("amps", [ROWS, HEADS])
        sine = sb("sine", [ROWS, HEADS])
        sine_sq = sb("sine_sq", [ROWS, HEADS])
        cosine = sb("cosine", [ROWS, HEADS])
        overlap = sb("overlap", [ROWS, HEADS])
        tanh_over = sb("tanh_over", [ROWS, HEADS])
        tanh_int = sb("tanh_int", [ROWS, HEADS])
        v1 = sb("v1", [ROWS, HEADS, HEAD1 + 1])
        weightsT = sb("weightsT", [ROWS, HEADS, ROWS])
        den = sb("den", [ROWS, HEADS])
        den_inv = sb("den_inv", [ROWS, HEADS])
        ratio = sb("ratio", [ROWS, HEADS, HEAD1])
        ratio_sum = sb("ratio_sum", [ROWS, HEADS])
        centred = sb("centred", [ROWS, HEADS, HEAD1])
        centred_sq = sb("centred_sq", [ROWS, HEADS, HEAD1])
        sq_sum = sb("sq_sum", [ROWS, HEADS])
        spread_h = sb("spread_h", [ROWS, HEADS])
        rstd_h = sb("rstd_h", [ROWS, HEADS])
        att1 = sb("att1", [ROWS, HEADS, HEAD1])
        att1T = sb("att1T", [HALF + 1, 2, ROWS])
        h3 = sb("h3", [ROWS, 2, EMBED])

        stats3 = sb("stats3", [ROWS, 6])
        moments3 = sb("moments3", [ROWS, 2])
        spread3 = sb("spread3", [ROWS, 1])
        rstd3 = sb("rstd3", [ROWS, 1])
        norm3 = sb("norm3", [ROWS, EMBED])
        norm3T = sb("norm3T", [HALF + 1, 2, ROWS])
        hid1T = sb("hid1T", [HIDDEN1, ROWS])
        h3_beta = sb("h3_beta", [ROWS, EMBED])
        stats4 = sb("stats4", [ROWS, 6])
        moments4 = sb("moments4", [ROWS, 2])
        spread4 = sb("spread4", [ROWS, 1])
        rstd4 = sb("rstd4", [ROWS, 1])
        scaled4 = sb("scaled4", [ROWS, EMBED])
        result = sb("result", [ROWS, 2, EMBED])
        pad_pool = sb("pad_pool", [128, 1])
        pad_act = sb("pad_act", [128, 1])
        pad = sb("pad", [128, 1])

        bank = {n: [ctx.enter_context(nc.psum_tensor(f"bank_{n}{i}", [128, 512], F32)) for i in range(2)]
                for n in ("embed", "att", "ffn", "lin")}
        E0, E1 = bank["embed"]
        A0, A1 = bank["att"]
        M0, M1 = bank["ffn"]
        L0, L1 = bank["lin"]

        step_names = """
            strips_cut patches0 patches1 patchT0 patchT1 embedded h0_copied stats0 moments0 spread0 rstd0
            norm0 norm0_turned norm0T v_half0 v_half1 v_copied0 v_copied1
            qk_done0 qk_done1 qk_done2 qk_copied0 qk_copied1 qk_copied2
            dots0 dots1 dots2 dots3 packed0 packed1 packed2 packed3 shifted expd probs
            widened0 widened1 widened2 turned0 turned1 turned2 probsT0 probsT1 probsT2 att_done0 att_done1 att_copied0 att_copied1
            proj0 h1
            moments1 rstd1 unit_in half_c2 big_in int_in in_turned in_copied gate_done up_done tanh_gate
            product scaled square_sum rms_inv big_out int_out out_turned out_copied down_done h2
            moments2 rstd2 norms2 norms_turned norms_copied qk1 hid relu_qk feat_q feat_k_all feat_k
            tanh_hid hidT params tanh_par overlap tanh_over tanh_int v1
            a_done0 a_done1 a_done2 a_masked0 a_masked1 a_masked2 num centred centred_sq sq_sum rstd_h
            att1 att1_turned att1_copied proj1 h3
            moments3 rstd3 norm3 norm3_turned norm3_copied hid1 hid1_copied h3_beta out4
            moments4 rstd4 scaled4 result
        """.split()
        S = {n: sem("s_" + n) for n in step_names}
        RUN = {n: sem("run_" + n) for n in "v_att v_ffn v_lin v_last p_ffn p_lin p_last".split()}
        strips_in = [sem("strips_in0"), sem("strips_in1")]
        stored = [sem("stored0"), sem("stored1")]
        ld_const, ld_tok, ld_qkv, ld_ffn, ld_lin, ld_late = (sem("ld_" + n) for n in
                                                            ("const", "tok", "qkv", "ffn", "lin", "late"))
        setup_pe, setup_turned, setup_dve, setup_sums, setup_ternary, setup_act, setup_pool, setup_row = (
            sem("setup_" + n) for n in ("pe", "turned", "dve", "sums", "ternary", "act", "pool", "row"))
        ready = sem("ready")
        READY = 2
        block = ctx.enter_context(nc.Block())

        def after(eng, semaphore, count):
            if not isinstance(count, int) or count > 0:
                eng.wait_ge(semaphore, count)

        def chain_of(eng, semaphore, links):
            count = [0]

            def then(g, instruction):
                count[0] = count[0] % links + 1
                instruction.then_inc(semaphore, 1)
                eng.wait_ge(semaphore, g * links + count[0])
            return then

        def iterations(eng, run):
            first = STAGES - 1 + (STAGES - 1) % 2
            end = first + (GROUPS - first) // 2 * 2
            for i in range(first):
                run(i, i % 2, [0 <= i - n < GROUPS for n in range(STAGES)])
            with eng.Fori(0, (end - first) // 2) as pair:
                run(2 * pair + first, 0, [True] * STAGES)
                run(2 * pair + (first + 1), 1, [True] * STAGES)
            for i in range(end, STEPS):
                run(i, i % 2, [0 <= i - n < GROUPS for n in range(STAGES)])

        def in_turn(i, parity, active, steps):
            for stage, step in steps:
                if active[stage]:
                    step(i - stage, (parity + stage) % 2)

        def row(ap):
            return ap.rearrange("(o n) -> o n", o=1)

        def parts(tile, n):
            return tile[:, 0:n * ROWS].rearrange("p (n r) -> p n r", n=n)

        @block.sync
        def _(sp):
            all_strips = a["x"].rearrange("b c (y r) w -> (b c y) (r w)", r=PATCH)

            def load(semaphore, dst, src):
                sp.dma_start(dst, src).then_inc(semaphore, 16)

            def load_column(semaphore, dst, src):
                sp.dma_start(dst, src, allow_slow_non_contiguous=True).then_inc(semaphore, 16)

            def load_strips(g, p):
                after(sp, S["strips_cut"], g - 1)
                first = g * PER if not isinstance(g, int) else min(g * PER, LAST_IMAGE)
                sp.dma_start(strips[:, p].rearrange("s r w -> s (r w)"),
                             all_strips[bass.ds(first * CHANNELS * GRID, STRIPS), :]).then_inc(strips_in[p], 16)

            load(ld_const, consts[:, :], table)
            load(ld_tok, w_tok_raw[:, :, :], a["L0_tok_W"].rearrange("(k p) n -> p k n", k=2))
            load(ld_tok, start_rows[0:1, :], row(a["L0_tok_b"]))
            load(ld_tok, start_rows[1:2, :], a["cls_tok"].rearrange("a b n -> (a b) n"))
            load_strips(0, 0)
            load(ld_qkv, w_qkv0[:, :, :], a["L0_attn_w_qkv"].rearrange("(k p) n -> p k n", k=2))
            load(ld_qkv, scale_b[:, :], a["L0_attn_scale"].partition_broadcast(HALF))
            load_strips(1, 1)
            load(ld_ffn, w_in_raw[:, :, :], a["L0_ffn_w_in"].rearrange("(k p) n -> p k n", p=128))
            load(ld_ffn, w_out_raw[:, :, :], a["L0_ffn_w_out"].rearrange("(k p) n -> p k n", k=2))
            load(ld_lin, w_qkv1_raw[:, :, :], a["L1_attn_Wqkv"].rearrange("(k p) n -> p k n", k=2))
            load_column(ld_lin, ln_wb[:, :, 0], a["L1_attn_ln_w"].rearrange("(k p) -> p k", k=2))
            load_column(ld_lin, ln_wb[:, :, 1], a["L1_attn_ln_b"].rearrange("(k p) -> p k", k=2))
            load(ld_lin, b_qkv1[:, :], row(a["L1_attn_bqkv"]))
            load(ld_lin, w_g2[:, :, :], a["L1_attn_Wb2"].rearrange("p (h n) -> p h n", n=GATES))
            load(ld_lin, temp[:, :], a["L1_attn_temperature"].partition_broadcast(ROWS))
            load(ld_lin, w_p1_raw[:, :, :], a["L1_attn_Wproj"].rearrange("(k p) n -> p k n", k=2))
            load(ld_lin, b_p1[:, :], row(a["L1_attn_bproj"]))
            for h in range(HALF // HEAD1):
                load_column(ld_lin, mn_wb[h * HEAD1:(h + 1) * HEAD1, 0:1], a["L1_attn_mn_w"].rearrange("(n o) -> n o", o=1))
                load_column(ld_lin, mn_wb[h * HEAD1:(h + 1) * HEAD1, 1:2], a["L1_attn_mn_b"].rearrange("(n o) -> n o", o=1))
            load(ld_lin, w1_raw[:, :], a["L1_ffn_W1"])
            load(ld_lin, w2_raw[:, :, :], a["L1_ffn_W2"].rearrange("(k p) n -> p k n", k=2))
            load(ld_lin, wo_raw[:, :, :], a["L1_ffn_Wo"].rearrange("(k p) n -> p k n", k=2))
            load_column(ld_lin, b2_col[:, :], a["L1_ffn_b2"].rearrange("(k p) -> p k", k=2))
            load(ld_lin, bo[:, :], row(a["L1_ffn_bo"]))
            load(ld_late, w_o0[:, :, :], a["L0_attn_w_out"].rearrange("(k p) n -> p k n", p=128))
            load(ld_late, b_o0[:, :], row(a["L0_attn_b_out"]))
            load(ld_late, g_in[:, :], a["L0_ffn_g_in"].partition_broadcast(ROWS))
            load(ld_late, g_out[:, :], a["L0_ffn_g_out"].partition_broadcast(ROWS))
            load(ld_late, w_g1[:, :, :], a["L1_attn_Wb1"].rearrange("(k p) n -> p k n", k=2))
            load(ld_late, gamma[:, :], a["L1_ffn_gamma"].partition_broadcast(ROWS))
            load(ld_late, beta[:, :], a["L1_ffn_beta"].partition_broadcast(ROWS))
            load(ld_late, w1[HALF:HALF + 1, 0, :], row(a["L1_ffn_b1"]))
            sp.wait_ge(setup_row, 1)
            load(ld_late, w_qkv1[HALF:HALF + 1, 0, :], b_qkv1[:, :])
            sp.wait_ge(setup_row, 2)
            load(ld_late, w_p1[HALF:HALF + 1, 0, :], b_p1[:, :])

            for g in range(2, 4):
                load_strips(g, g % 2)
            with sp.Fori(2, GROUPS // 2) as pair:
                load_strips(2 * pair, 0)
                load_strips(2 * pair + 1, 1)
            load_strips(GROUPS - 1, (GROUPS - 1) % 2)

        @block.gpsimd
        def _(pool):
            pool.memset(ones[:, :], 1.0)
            pool.memset(minus_half[:, :], -0.5)
            for n, value in enumerate((1.0 + EPS_RMS, EPS * EPS_RMS, 1.0, 1.0 + EPS, EPS, EPS * EPS, EPS, EPS_RMS)):
                pool.memset(gain_eps[:, n:n + 1], value)
            gain1, eps1, gain2, eps2 = gain_eps[0:ROWS, 0:1], gain_eps[0:ROWS, 1:2], gain_eps[0:ROWS, 2:4], gain_eps[0:ROWS, 4:6]
            eps_ln, eps_rms = gain_eps[0:ROWS, 6:7], gain_eps[0:ROWS, 7:8]
            pool.memset(eps_head[:, :], HEAD1 * EPS)
            for n, c in enumerate(sine_coefficients()):
                pool.memset(sine_terms[:, n, :], c)
            pool.memset(pad_pool[:, :], 0.0)
            pool.memset(patchT[:, :, :], 0.0)
            pool.memset(scores[:, :, :], FILLER)
            pool.memset(v1[:, :, :], 1.0)
            pool.memset(norms2T[:, :, :], 1.0)
            pool.memset(att1T[:, :, :], 1.0)
            pool.memset(norm3T[:, :, :], 1.0).then_inc(setup_pool, 1)
            pool.wait_ge(setup_pool, 1)
            pool.wait_ge(ready, READY)
            pool.wait_ge(ld_late, 16 * 10)

            ffn_chain = chain_of(pool, RUN["p_ffn"], 3)
            lin_chain = chain_of(pool, RUN["p_lin"], 2 * SINE_ORDER + 8)
            last_chain = chain_of(pool, RUN["p_last"], 2)

            def rstd(g, chain, rstd_ready, var, spread, rstd_out, eps):
                chain(g, pool.tensor_tensor(spread, var, eps, ALU.add))
                pool.tensor_tensor(rstd_out, spread, minus_half[0:ROWS, 0:spread.shape[1]], ALU.pow) \
                    .then_inc(rstd_ready, 1)

            def p_strips(g, p):
                pool.wait_ge(strips_in[p], 16 * (g // 2 + 1) if isinstance(g, int) else 8 * (g - p) + 16)
                after(pool, S["patches1"], g)
                pool.tensor_tensor(pad_pool[:, :], pad_pool[:, :], ones[:, 0:1], ALU.mult)
                pool.tensor_copy(patches[:, :, :].rearrange("p x (r c) -> p x r c", r=PATCH),
                                 strips[:, p].rearrange("p r (x c) -> p x r c", x=GRID)).then_inc(S["strips_cut"], 1)

            def p_rstd0(g, p):
                pool.wait_ge(S["moments0"], g + 1)
                rstd(g, chain_of(pool, S["spread0"], 1), S["rstd0"], moments0[:, 1:2], spread0[:, :], rstd0[:, :], eps_ln)

            def p_rstd1(g, p):
                pool.wait_ge(S["moments1"], g + 1)
                ffn_chain(g, pool.tensor_tensor(spread1[:, 0:1], moments1[:, 1:2], gain1, ALU.mult))
                rstd(g, ffn_chain, S["rstd1"], spread1[:, 0:1], spread1[:, 1:2], rstd1[:, :], eps1)

            def p_rms(g, p):
                pool.wait_ge(S["square_sum"], g + 1)
                rstd(g, ffn_chain, S["rms_inv"], square_sum[:, :], mean_square[:, :], rms_inv[:, :], eps_rms)

            def p_scaled(g, p):
                pool.wait_ge(S["product"], g + 1)
                pool.tensor_tensor(scaled[:, :], product[:, :], g_out[:, :], ALU.mult).then_inc(S["scaled"], 1)

            def p_rstd2(g, p):
                pool.wait_ge(S["moments2"], g + 1)
                lin_chain(g, pool.tensor_tensor(spread2[:, 0], moments2[:, 1:2].to_broadcast([ROWS, 2]), gain2, ALU.mult))
                rstd(g, lin_chain, S["rstd2"], spread2[:, 0], spread2[:, 1], rstd2[:, :], eps2)

            def p_feat_k(g, p):
                pool.wait_ge(S["feat_k_all"], g + 1)
                for odd in range(2):
                    keep = consts[0:HALF, C_PARITY + odd:C_PARITY + odd + 1].unsqueeze(2).to_broadcast([HALF, 2, ROWS])
                    last = pool.tensor_tensor(feat_k[:, odd], feat_qk[:, 2:4, :], keep, ALU.mult)
                last.then_inc(S["feat_k"], 1)

            def p_gate(g, p):
                pool.wait_ge(S["tanh_par"], g + 1)
                for n in range(2):
                    pool.tensor_tensor(amp[:, n], tanh_par[:, :, 2 * n], ones[0:ROWS, 0:HEADS], ALU.add)
                lin_chain(g, pool.tensor_tensor(wave[:, :], tanh_par[:, :, 1], tanh_par[:, :, 3], ALU.subtract))
                pool.tensor_tensor(amps[:, :], amp[:, 0], amp[:, 1], ALU.mult)
                lin_chain(g, pool.tensor_tensor(wave_sq[:, :], wave[:, :], wave[:, :], ALU.mult))
                lin_chain(g, pool.tensor_tensor(poly[:, 1], sine_terms[0:ROWS, 0], wave_sq[:, :], ALU.mult))
                for n in range(1, SINE_ORDER + 1):
                    lin_chain(g, pool.tensor_tensor(poly[:, 0], poly[:, 1], sine_terms[0:ROWS, n], ALU.add))
                    if n < SINE_ORDER:
                        lin_chain(g, pool.tensor_tensor(poly[:, 1], poly[:, 0], wave_sq[:, :], ALU.mult))
                lin_chain(g, pool.tensor_tensor(sine[:, :], poly[:, 0], wave[:, :], ALU.mult))
                lin_chain(g, pool.tensor_tensor(sine_sq[:, :], sine[:, :], sine[:, :], ALU.mult))
                lin_chain(g, pool.tensor_tensor(cosine[:, :], ones[0:ROWS, 0:HEADS], sine_sq[:, :], ALU.subtract))
                pool.tensor_tensor(overlap[:, :], cosine[:, :], amps[:, :], ALU.mult).then_inc(S["overlap"], 1)

            def p_centred_sq(g, p):
                pool.wait_ge(S["centred"], g + 1)
                pool.tensor_tensor(centred_sq[:, :, :], centred[:, :, :], centred[:, :, :], ALU.mult) \
                    .then_inc(S["centred_sq"], 1)

            def p_rstd_h(g, p):
                pool.wait_ge(S["sq_sum"], g + 1)
                rstd(g, lin_chain, S["rstd_h"], sq_sum[:, :], spread_h[:, :], rstd_h[:, :], eps_head[0:ROWS, :])

            def p_rstd3(g, p):
                pool.wait_ge(S["moments3"], g + 1)
                rstd(g, last_chain, S["rstd3"], moments3[:, 1:2], spread3[:, :], rstd3[:, :], eps_ln)

            def p_h3_beta(g, p):
                pool.wait_ge(S["h3"], g + 1)
                pool.tensor_tensor(h3_beta[:, :], h3[:, p], beta[:, :], ALU.add).then_inc(S["h3_beta"], 1)

            def p_rstd4(g, p):
                pool.wait_ge(S["moments4"], g + 1)
                rstd(g, last_chain, S["rstd4"], moments4[:, 1:2], spread4[:, :], rstd4[:, :], eps_ln)

            iterations(pool, lambda i, parity, active: in_turn(i, parity, active, [
                (4, p_rstd3), (3, p_rstd2), (0, p_strips), (0, p_rstd0), (4, p_h3_beta), (3, p_feat_k), (4, p_rstd4),
                (3, p_gate), (2, p_rstd1), (2, p_scaled), (2, p_rms), (3, p_centred_sq), (3, p_rstd_h),
            ]))

        @block.vector
        def _(dve):
            done = [0]

            def link(instruction):
                done[0] += 1
                instruction.then_inc(setup_dve, 1)
                dve.wait_ge(setup_dve, done[0])

            dve.wait_ge(ld_const, 16)
            dve.wait_ge(setup_pool, 1)
            dve.tensor_copy(ident_b[:, :], ident)
            link(dve.tensor_copy(score_mask_b[:, :], consts[0:ROWS, C_SCORE:C_SCORE + ROWS]))
            dve.wait_ge(ld_qkv, 32)
            link(dve.tensor_scalar(scale_b[:, :], scale_b[:, :], -1.0, None, ALU.mult))
            for k in range(2):
                wq = w_qkv0[:, k, 0:INNER].rearrange("p (h d) -> p h d", h=HEADS)
                link(dve.tensor_tensor(wq, wq, scale_b[:, :].unsqueeze(2).to_broadcast([HALF, HEADS, HEAD0]), ALU.mult))
            dve.wait_ge(ld_ffn, 32)
            link(dve.memset(abs_sums[:, :], 0.0))
            flat_in = w_in_raw[:, :, :].rearrange("p k n -> p (k n)")
            flat_out = w_out_raw[:, :, :].rearrange("p k n -> p (k n)")
            dve.tensor_reduce(abs_sums[:, 0:1], flat_in, X, ALU.add, apply_absolute_value=True)
            dve.tensor_reduce(abs_sums[0:HALF, 1:2], flat_out, X, ALU.add, apply_absolute_value=True) \
                .then_inc(setup_sums, 1)
            dve.wait_ge(setup_pe, 1)
            link(dve.tensor_scalar(w_scale[:, 0:1], M0[:, 0:1], 1.0 / (2 * HIDDEN0 * EMBED), EPS_QUANT, ALU.mult, ALU.max))
            link(dve.tensor_scalar(w_scale[:, 1:2], M0[:, 1:2], 1.0 / (HIDDEN0 * EMBED), EPS_QUANT, ALU.mult, ALU.max))
            link(dve.reciprocal(w_scale_inv[:, :], w_scale[:, :]))
            link(dve.tensor_scalar(w_scale_127[:, :], w_scale[:, :], 1.0 / 127.0, None, ALU.mult))
            for flat, n, q in ((flat_in, 0, w_in_q[:, :, :]), (flat_out, 1, w_out_q[:, :, :])):
                rows = flat.shape[0]
                link(dve.tensor_scalar(flat, flat, w_scale_inv[0:rows, n:n + 1], ROUND, ALU.mult, ALU.add))
                link(dve.tensor_scalar(flat, flat, -ROUND, 1.0, ALU.add, ALU.min))
                link(dve.tensor_scalar(q.rearrange("p k n -> p (k n)"), flat, -1.0, None, ALU.max))
            link(dve.memset(pad[:, :], 0.0))
            dve.memset(pad[:, :], 0.0).then_inc(setup_ternary, 1)
            dve.wait_ge(ld_lin, 16 * 25)
            for k in range(2):
                link(dve.tensor_scalar(w_qkv1[0:HALF, k, :], w_qkv1_raw[:, k, :], ln_wb[:, k, 0:1], None, ALU.mult))
                link(dve.tensor_scalar(w_p1[0:HALF, k, :], w_p1_raw[:, k, :], mn_wb[:, 0:1], HEAD1 ** 0.5, ALU.mult, ALU.mult))
            link(dve.tensor_scalar(w_g2[:, :, :], w_g2[:, :, :], 0.5, None, ALU.mult))
            for n in (0, 2):
                link(dve.tensor_scalar(w_g2[:, :, n], w_g2[:, :, n], 0.5, None, ALU.mult))
            link(dve.tensor_scalar(temp[:, :], temp[:, :], 0.1, 2.0, ALU.max, ALU.min))
            link(dve.tensor_scalar(temp[:, :], temp[:, :], 0.5, None, ALU.mult))
            dve.wait_ge(setup_pe, 2)
            dve.tensor_tensor(b_qkv1[:, 0:384], L0[0:1, 0:384], b_qkv1[:, 0:384], ALU.add)
            dve.tensor_tensor(b_qkv1[:, 384:576], L1[0:1, 0:192], b_qkv1[:, 384:576], ALU.add).then_inc(setup_row, 1)
            dve.tensor_tensor(b_p1[:, :], L1[0:1, 192:384], b_p1[:, :], ALU.add).then_inc(setup_row, 1)
            dve.wait_ge(setup_pe, 3)
            dve.tensor_tensor(b2o[:, :], A1[0:1, 192:384], bo[:, :], ALU.add)
            link(dve.tensor_copy(w2o[:, :], A1[:, 0:192]))
            dve.wait_ge(setup_row, 2)
            link(dve.memset(pad[:, :], 0.0))
            dve.memset(pad[:, :], 0.0).then_inc(ready, 1)
            dve.wait_ge(ready, READY)
            dve.wait_ge(ld_late, 16 * 10)

            att_chain = chain_of(dve, RUN["v_att"], 7)
            ffn_chain = chain_of(dve, RUN["v_ffn"], 12)
            lin_chain = chain_of(dve, RUN["v_lin"], 5)
            last_chain = chain_of(dve, RUN["v_last"], 2)

            def stats(g, chain, stats_tile, moments, moments_ready, src):
                chain(g, dve.bn_stats(stats_tile[:, :], src))
                dve.memset(pad[0:ROWS, :], 0.0)
                dve.bn_aggr(moments[:, :], stats_tile[:, :]).then_inc(moments_ready, 1)

            def v_stats0(g, p):
                dve.wait_ge(S["h0_copied"], g + 1)
                stats(g, chain_of(dve, S["stats0"], 1), stats0, moments0, S["moments0"], h0[:, p])

            def v_norm0(g, p):
                dve.wait_ge(S["rstd0"], g + 1)
                after(dve, S["norm0_turned"], g)
                dve.tensor_scalar(norm0[:, :], h0[:, p], moments0[:, 0:1], rstd0[:, 0:1],
                                  ALU.subtract, ALU.mult).then_inc(S["norm0"], 1)

            def v_pack(f, src):
                def step(g, p):
                    dve.wait_ge(dots[f], g + 1)
                    dve.tensor_reduce(scores[:, 3 * f:3 * f + 3, TOKENS - 1::-1],
                                      src[0:ROWS, 0:3 * ROWS].rearrange("p (h b j) -> p h j b", h=3, b=PER),
                                      X, ALU.max).then_inc(packed[f], 1)
                return step

            def v_top(g, p):
                for f in range(4):
                    dve.wait_ge(packed[f], g + 1)
                dve.tensor_reduce(score_sum[:, :], scores[:, :, 0:TOKENS].rearrange("p h j -> p j h"), X, ALU.add)
                for h in range(HEADS):
                    last = dve.max(top[:, h, :], scores[:, h, 0:TOKENS])
                att_chain(g, last)
                att_chain(g, dve.memset(top[:, :, DROP + 1:8], FILLER))

            def v_drop(g, p):
                dve.memset(pad[0:ROWS, :], 0.0)
                for h in range(HEADS):
                    last = dve.match_replace(kept[:, h, :], top[:, h, :], scores[:, h, :], BIG)
                att_chain(g, last)

            def v_mix(g, p):
                att_chain(g, dve.scalar_tensor_tensor(
                    mixed[:, :, :], score_sum[:, :].unsqueeze(1).to_broadcast([ROWS, HEADS, TOKENS]),
                    1.0 / HEADS, kept[:, :, 0:TOKENS], ALU.mult, ALU.add))
                att_chain(g, dve.tensor_reduce(least[:, :], mixed[:, :, :], X, ALU.min))
                dve.tensor_tensor(shifted[:, :, :], mixed[:, :, :],
                                  least[:, :].unsqueeze(2).to_broadcast([ROWS, HEADS, TOKENS]),
                                  ALU.subtract).then_inc(S["shifted"], 1)

            def v_probs(g, p):
                dve.wait_ge(S["expd"], g + 1)
                att_chain(g, dve.tensor_reduce(exp_sum[:, :], expd[:, :, :], X, ALU.add))
                att_chain(g, dve.reciprocal(exp_inv[:, :], exp_sum[:, :]))
                dve.tensor_tensor(probs[:, :, :], expd[:, :, ::-1],
                                  exp_inv[:, :].unsqueeze(2).to_broadcast([ROWS, HEADS, TOKENS]),
                                  ALU.mult).then_inc(S["probs"], 1)

            def masked(turned, mask, dst, ready_sem, src):
                def step(g, p):
                    dve.wait_ge(turned, g + 1)
                    dve.tensor_tensor(dst, parts(src, 4)[0:ROWS], mask.unsqueeze(1).to_broadcast([ROWS, 4, ROWS]),
                                      ALU.mult).then_inc(ready_sem, 1)
                return step

            def v_wide(f):
                def step(g, p):
                    dve.wait_ge(S["probs"], g + 1)
                    if f == 0:
                        after(dve, S["turned2"], g)
                    dve.tensor_tensor(
                        wide[:, 4 * f:4 * f + 4], probs[:, 4 * f:4 * f + 4, :].unsqueeze(2).to_broadcast([ROWS, 4, PER, TOKENS]),
                        block_mask.rearrange("p (b j) -> p b j", b=PER).unsqueeze(1).to_broadcast([ROWS, 4, PER, TOKENS]),
                        ALU.mult).then_inc((S["widened0"], S["widened1"], S["widened2"])[f], 1)
                return step

            def v_h1(g, p):
                dve.wait_ge(S["proj0"], g + 1)
                dve.tensor_tensor(h1[:, p], A1[0:ROWS, 0:EMBED], h0[:, p], ALU.add).then_inc(S["h1"], 1)

            def v_u_in(g, p):
                dve.wait_ge(S["h1"], g + 1)
                stats(g, ffn_chain, stats1, moments1, S["moments1"], h1[:, p])
                dve.wait_ge(S["moments1"], g + 1)
                ffn_chain(g, dve.scalar_tensor_tensor(u_in[:, :], h1[:, p], moments1[:, 0:1], g_in[:, :],
                                                      ALU.subtract, ALU.mult))
                ffn_chain(g, dve.tensor_reduce(umax_in[:, :], u_in[:, :], X, ALU.max, apply_absolute_value=True))

            def v_big_in(g, p):
                dve.wait_ge(S["rstd1"], g + 1)
                ffn_chain(g, dve.tensor_scalar(amax_in[:, :], umax_in[:, :], rstd1[:, 0:1], EPS_QUANT, ALU.mult, ALU.max))
                dve.tensor_scalar(unit_in[:, 1:2], amax_in[:, :], w_scale_127[0:ROWS, 0:1], None, ALU.mult)
                dve.tensor_scalar(unit_in[:, 0:1], amax_in[:, :], w_scale_127[0:ROWS, 0:1], 0.5, ALU.mult, ALU.mult) \
                    .then_inc(S["unit_in"], 1)
                ffn_chain(g, dve.reciprocal(ainv_in[:, :], amax_in[:, :]))
                ffn_chain(g, dve.tensor_scalar(quant_in[:, :], ainv_in[:, :], rstd1[:, 0:1], 127.0, ALU.mult, ALU.mult))
                dve.tensor_scalar(big_in[:, :], u_in[:, :], quant_in[:, 0:1], ROUND, ALU.mult, ALU.add) \
                    .then_inc(S["big_in"], 1)
                dve.tensor_scalar(half_c2[:, 0:1], unit_in[:, 0:1], unit_in[:, 1:2], None, ALU.mult)
                dve.tensor_scalar(half_c2[:, 1:2], unit_in[:, 0:1], unit_in[:, 1:2], HIDDEN0 ** -0.5, ALU.mult, ALU.mult) \
                    .then_inc(S["half_c2"], 1)

            def v_gated(g, p):
                dve.wait_ge(S["tanh_gate"], g + 1)
                ffn_chain(g, dve.scalar_tensor_tensor(gated[:, :], tanh_gate[:, :], 1.0, M1[0:ROWS, :], ALU.add, ALU.mult))
                dve.wait_ge(S["up_done"], g + 1)
                dve.tensor_tensor(product[:, :], M0[0:ROWS, :], gated[:, :], ALU.mult).then_inc(S["product"], 1)

            def v_big_out(g, p):
                dve.wait_ge(S["scaled"], g + 1)
                ffn_chain(g, dve.tensor_reduce(umax_out[:, :], scaled[:, :], X, ALU.max, apply_absolute_value=True))
                dve.wait_ge(S["rms_inv"], g + 1)
                ffn_chain(g, dve.tensor_scalar(row_gain[:, :], rms_inv[:, :], half_c2[:, 0:1], None, ALU.mult))
                ffn_chain(g, dve.tensor_scalar(amax_out[:, :], umax_out[:, :], row_gain[:, 0:1], EPS_QUANT, ALU.mult, ALU.max))
                dve.tensor_scalar(unit_out[:, :], amax_out[:, :], w_scale_127[0:ROWS, 1:2], None, ALU.mult)
                ffn_chain(g, dve.reciprocal(ainv_out[:, :], amax_out[:, :]))
                ffn_chain(g, dve.tensor_scalar(quant_out[:, :], ainv_out[:, :], row_gain[:, 0:1], 127.0, ALU.mult, ALU.mult))
                dve.tensor_scalar(big_out[:, :], scaled[:, :], quant_out[:, 0:1], ROUND, ALU.mult, ALU.add) \
                    .then_inc(S["big_out"], 1)

            def v_h2(g, p):
                dve.wait_ge(S["down_done"], g + 1)
                dve.scalar_tensor_tensor(h2[:, p], M0[0:ROWS, 0:EMBED], unit_out[:, 0:1], h1[:, p],
                                         ALU.mult, ALU.add).then_inc(S["h2"], 1)

            def v_stats2(g, p):
                dve.wait_ge(S["h2"], g + 1)
                stats(g, lin_chain, stats2, moments2, S["moments2"], h2[:, p])

            def v_norms2(g, p):
                dve.wait_ge(S["rstd2"], g + 1)
                for n in range(2):
                    last = dve.tensor_scalar(norms2[:, n], h2[:, p], moments2[:, 0:1], rstd2[:, n:n + 1],
                                             ALU.subtract, ALU.mult)
                last.then_inc(S["norms2"], 1)

            def v_hidT(g, p):
                dve.wait_ge(S["tanh_hid"], g + 1)
                dve.scalar_tensor_tensor(hidT[:, :], tanh_hid[:, :], 1.0, L0[:, 0:ROWS], ALU.add, ALU.mult) \
                    .then_inc(S["hidT"], 1)

            def v_feat(g, p):
                dve.wait_ge(S["relu_qk"], g + 1)
                for n, ready_sem in ((2, S["feat_k_all"]), (0, S["feat_q"])):
                    dve.scalar_tensor_tensor(feat_qk[:, n:n + 2, :], exp_qk[:, n:n + 2, :], 1.0, relu_qk[:, n:n + 2, :],
                                             ALU.min, ALU.add).then_inc(ready_sem, 1)

            def v_v1(g, p):
                dve.wait_ge(S["tanh_int"], g + 1)
                dve.scalar_tensor_tensor(v1[:, :, 0:HEAD1], tanh_int[:, :].unsqueeze(2).to_broadcast([ROWS, HEADS, HEAD1]), 3.0,
                                         L0[0:ROWS, 128:128 + EMBED].rearrange("p (h d) -> p h d", h=HEADS),
                                         ALU.add, ALU.mult).then_inc(S["v1"], 1)

            def v_ratio(g, p):
                num = L0[0:ROWS, 0:HEADS * (HEAD1 + 1)].rearrange("p (h d) -> p h d", h=HEADS)
                dve.wait_ge(S["num"], g + 1)
                lin_chain(g, dve.tensor_scalar(den[:, :], num[:, :, HEAD1], 2.0, 2 * EPS_DEN, ALU.mult, ALU.add))
                lin_chain(g, dve.reciprocal(den_inv[:, :], den[:, :]))
                lin_chain(g, dve.tensor_tensor(ratio[:, :, :], num[:, :, 0:HEAD1],
                                               den_inv[:, :].unsqueeze(2).to_broadcast([ROWS, HEADS, HEAD1]), ALU.mult))
                lin_chain(g, dve.tensor_reduce(ratio_sum[:, :], ratio[:, :, :], X, ALU.add))
                dve.scalar_tensor_tensor(centred[:, :, :], ratio_sum[:, :].unsqueeze(2).to_broadcast([ROWS, HEADS, HEAD1]),
                                         -1.0 / HEAD1, ratio[:, :, :], ALU.mult, ALU.add).then_inc(S["centred"], 1)

            def v_sq_sum(g, p):
                dve.wait_ge(S["centred_sq"], g + 1)
                dve.tensor_reduce(sq_sum[:, :], centred_sq[:, :, :], X, ALU.add).then_inc(S["sq_sum"], 1)

            def v_att1(g, p):
                dve.wait_ge(S["rstd_h"], g + 1)
                dve.tensor_tensor(att1[:, :, :], centred[:, :, :],
                                  rstd_h[:, :].unsqueeze(2).to_broadcast([ROWS, HEADS, HEAD1]), ALU.mult) \
                    .then_inc(S["att1"], 1)

            def v_h3(g, p):
                dve.wait_ge(S["proj1"], g + 1)
                dve.tensor_tensor(h3[:, p], L0[0:ROWS, 256:256 + EMBED], h2[:, p], ALU.add).then_inc(S["h3"], 1)

            def v_stats3(g, p):
                dve.wait_ge(S["h3"], g + 1)
                stats(g, last_chain, stats3, moments3, S["moments3"], h3[:, p])

            def v_norm3(g, p):
                dve.wait_ge(S["rstd3"], g + 1)
                dve.tensor_scalar(norm3[:, :], h3[:, p], moments3[:, 0:1], rstd3[:, 0:1],
                                  ALU.subtract, ALU.mult).then_inc(S["norm3"], 1)

            def v_stats4(g, p):
                dve.wait_ge(S["out4"], g + 1)
                stats(g, last_chain, stats4, moments4, S["moments4"], M1[0:ROWS, 0:EMBED])
                dve.wait_ge(S["moments4"], g + 1)
                dve.scalar_tensor_tensor(scaled4[:, :], M1[0:ROWS, 0:EMBED], moments4[:, 0:1], gamma[:, :],
                                         ALU.subtract, ALU.mult).then_inc(S["scaled4"], 1)

            def v_result(g, p):
                dve.wait_ge(S["rstd4"], g + 1)
                dve.wait_ge(S["scaled4"], g + 1)
                dve.wait_ge(S["h3_beta"], g + 1)
                after(dve, stored[p], 16 * (g // 2) if isinstance(g, int) else 8 * (g - p))
                dve.scalar_tensor_tensor(result[:, p], scaled4[:, :], rstd4[:, 0:1], h3_beta[:, :],
                                         ALU.mult, ALU.add).then_inc(S["result"], 1)

            dots = [S["dots0"], S["dots1"], S["dots2"], S["dots3"]]
            packed = [S["packed0"], S["packed1"], S["packed2"], S["packed3"]]
            v_causal = [masked(t, causal_mask, weightsT[:, 4 * f:4 * f + 4, :], m, src) for f, (t, m, src) in enumerate(
                ((S["a_done0"], S["a_masked0"], L1), (S["a_done1"], S["a_masked1"], L0), (S["a_done2"], S["a_masked2"], L1)))]

            iterations(dve, lambda i, parity, active: in_turn(i, parity, active, [
                (4, v_stats3), (3, v_stats2), (4, v_norm3), (3, v_norms2),
                (1, v_pack(0, A0)), (1, v_pack(1, A1)), (1, v_pack(2, A0)), (1, v_pack(3, A1)), (1, v_top),
                (0, v_stats0), (0, v_norm0), (1, v_drop), (3, v_hidT), (3, v_feat), (4, v_stats4), (4, v_result),
                (1, v_mix), (2, v_u_in), (3, v_v1), (3, v_causal[0]), (2, v_big_in), (1, v_probs),
                (3, v_causal[1]), (1, v_wide(0)), (1, v_wide(1)), (3, v_causal[2]), (1, v_wide(2)), (3, v_ratio),
                (2, v_gated), (3, v_sq_sum), (2, v_big_out), (3, v_att1), (1, v_h1), (3, v_h3), (2, v_h2),
            ]))

        @block.scalar
        def _(act):
            copied = [0]

            def evac(dst, src, turned):
                act.wait_ge(setup_turned, turned)
                act.copy(dst, src).then_inc(setup_act, 1)
                copied[0] += 1

            for k in range(0, CHUNKS, 2):
                evac(w_tok[:, k:k + 2, :], (E0 if k % 4 == 0 else E1)[:, 0:2 * EMBED].rearrange("p (k n) -> p k n", k=2), k // 2 + 1)
            evac(w1[0:HALF, :, :], L0[0:HALF, 0:2 * HIDDEN1].rearrange("p (k n) -> p k n", k=2), 4)
            evac(wo[:, :, :], L1[0:HALF, 0:2 * EMBED].rearrange("p (k n) -> p k n", k=2), 5)
            for n in range(4):
                src = (A0, A1)[n % 2][:, :].bitcast(BF16)[0:HALF, 0:512].rearrange("p (k n) -> p k n", k=2)
                evac(w_in[:, :, 256 * n:256 * n + 256], src, 6 + n)
            for n in range(2):
                src = (A0, A1)[n % 2][:, :].bitcast(BF16)[:, 0:2 * EMBED].rearrange("p (k n) -> p k n", k=2)
                evac(w_out[:, 2 * n:2 * n + 2, :], src, 10 + n)
            act.wait_ge(setup_act, copied[0])
            act.wait_ge(setup_pool, 1)
            act.copy(pad_act[:, :], ones[:, 0:1]).then_inc(ready, 1)
            act.wait_ge(ready, READY)

            def copy_step(waits, dst, src, done_sem):
                def step(g, p):
                    for w in waits:
                        act.wait_ge(w, g + 1)
                    act.copy(dst, src).then_inc(done_sem, 1)
                return step

            def a_patchT(n, bank_tile, turned, done_sem):
                def step(g, p):
                    act.wait_ge(turned, g + 1)
                    if n == 0:
                        after(act, S["embedded"], g)
                    act.copy(patchT[:, n::2, :].rearrange("p c (b t) -> p c b t", t=TOKENS)[:, :, :, 1:TOKENS],
                             bank_tile[:, 0:STRIPS * GRID].rearrange("p (b c t) -> p c b t", b=PER, c=CHANNELS)) \
                        .then_inc(done_sem, 1)
                return step

            def a_h0(g, p):
                act.wait_ge(S["embedded"], g + 1)
                after(act, S["h1"], g - 1)
                act.copy(h0[:, p], E0[0:ROWS, 0:EMBED]).then_inc(S["h0_copied"], 1)

            def a_norm0T(g, p):
                act.wait_ge(S["norm0_turned"], g + 1)
                act.copy(norm0T[:, :, :], parts(E1, 2)[0:HALF]).then_inc(S["norm0T"], 1)

            def a_v(n):
                def step(g, p):
                    act.wait_ge((S["v_half0"], S["v_half1"])[n], g + 1)
                    if n == 0:
                        after(act, S["att_done1"], g - 1)
                    act.copy(v0[:, p, n * 384:(n + 1) * 384], (E0, E1)[n][0:ROWS, 0:384]) \
                        .then_inc((S["v_copied0"], S["v_copied1"])[n], 1)
                return step

            def a_qk(n):
                def step(g, p):
                    act.wait_ge((S["qk_done0"], S["qk_done1"], S["qk_done2"])[n], g + 1)
                    if n == 0:
                        after(act, S["dots3"], g - 1)
                    act.copy(qkT[:, p, 4 * n:4 * n + 4, :], parts((E0, E1, E0)[n], 4)) \
                        .then_inc((S["qk_copied0"], S["qk_copied1"], S["qk_copied2"])[n], 1)
                return step

            def a_exp(g, p):
                act.wait_ge(S["shifted"], g + 1)
                act.activation(expd[:, :, :], shifted[:, :, :], ACT.Exp, scale=-1.0).then_inc(S["expd"], 1)

            a_probsT = [copy_step([(S["turned0"], S["turned1"], S["turned2"])[f]], probsT[:, 4 * f:4 * f + 4, :],
                                  parts((A0, A1, A0)[f], 4)[0:ROWS], (S["probsT0"], S["probsT1"], S["probsT2"])[f]) for f in range(3)]
            a_att = [copy_step([(S["att_done0"], S["att_done1"])[n]], att0T[:, 3 * n:3 * n + 3, :], parts((A1, A0)[n], 3),
                               (S["att_copied0"], S["att_copied1"])[n]) for n in range(2)]

            def a_int_in(g, p):
                act.wait_ge(S["big_in"], g + 1)
                act.activation(int_in[:, :], big_in[:, :], ACT.Copy, bias=-ROUND).then_inc(S["int_in"], 1)

            a_in_T = copy_step([S["in_turned"]], int_inT[:, :, :],
                               M0[:, :].bitcast(BF16)[0:HALF, 0:256].rearrange("p (k n) -> p k n", k=2)[:, :, 0:ROWS],
                               S["in_copied"])

            def a_tanh_gate(g, p):
                act.wait_ge(S["gate_done"], g + 1)
                act.wait_ge(S["unit_in"], g + 1)
                act.activation(tanh_gate[:, :], M1[0:ROWS, :], ACT.Tanh, scale=unit_in[:, 0:1]).then_inc(S["tanh_gate"], 1)

            def a_square(g, p):
                act.wait_ge(S["product"], g + 1)
                act.wait_ge(S["half_c2"], g + 1)
                act.activation(squares[:, :], product[:, :], ACT.Square, scale=half_c2[:, 1:2],
                               accum_out=square_sum[:, :]).then_inc(S["square_sum"], 1)

            def a_int_out(g, p):
                act.wait_ge(S["big_out"], g + 1)
                act.activation(int_out[:, :], big_out[:, :], ACT.Copy, bias=-ROUND).then_inc(S["int_out"], 1)

            a_out_T = copy_step([S["out_turned"]], int_outT[:, :, :],
                                M1[:, :].bitcast(BF16)[:, 0:512].rearrange("p (k n) -> p k n", k=4)[:, :, 0:ROWS],
                                S["out_copied"])

            a_norms_T = copy_step([S["norms_turned"]], norms2T[0:HALF, :, :], parts(L0, 4)[0:HALF], S["norms_copied"])

            def a_qk1(g, p):
                act.wait_ge(S["qk1"], g + 1)
                act.activation(exp_qk[:, :, :], parts(L1, 4)[0:HALF], ACT.Exp)
                act.activation(relu_qk[:, :, :], parts(L1, 4)[0:HALF], ACT.Relu).then_inc(S["relu_qk"], 1)

            def a_tanh_hid(g, p):
                act.wait_ge(S["hid"], g + 1)
                act.activation(tanh_hid[:, :], L0[:, 0:ROWS], ACT.Tanh, scale=0.5).then_inc(S["tanh_hid"], 1)

            def a_tanh_par(g, p):
                act.wait_ge(S["params"], g + 1)
                act.activation(tanh_par[:, :, :], L0[0:ROWS, 384:384 + HEADS * GATES].rearrange("p (h n) -> p h n", n=GATES),
                               ACT.Tanh).then_inc(S["tanh_par"], 1)

            def a_interference(g, p):
                act.wait_ge(S["overlap"], g + 1)
                act.activation(tanh_over[:, :], overlap[:, :], ACT.Tanh, scale=0.25).then_inc(S["tanh_over"], 1)
                act.wait_ge(S["tanh_over"], g + 1)
                act.activation(tanh_int[:, :], tanh_over[:, :], ACT.Tanh, scale=temp[:, 0:1]).then_inc(S["tanh_int"], 1)

            a_att1_T = copy_step([S["att1_turned"]], att1T[0:HALF, :, :], parts(L1, 2)[0:HALF], S["att1_copied"])

            a_norm3_T = copy_step([S["norm3_turned"]], norm3T[0:HALF, :, :], parts(M1, 2)[0:HALF], S["norm3_copied"])

            def a_hid1(g, p):
                act.wait_ge(S["hid1"], g + 1)
                act.activation(hid1T[:, :], M0[:, 0:ROWS], ACT.Relu).then_inc(S["hid1_copied"], 1)

            def a_store(g, p):
                act.wait_ge(S["result"], g + 1)
                if isinstance(g, int) and g == GROUPS - 1:
                    first = (GROUPS - 1) * PER
                    n = (IMAGES - first) * TOKENS
                    act.dma_start(out[first * TOKENS:IMAGES * TOKENS, :], result[ROWS - n:ROWS, p]).then_inc(stored[p], 16)
                else:
                    act.dma_start(out[bass.ds(g * ROWS, ROWS), :], result[:, p]).then_inc(stored[p], 16)

            iterations(act, lambda i, parity, active: in_turn(i, parity, active, [
                (0, a_patchT(0, E0, S["patches0"], S["patchT0"])), (0, a_patchT(1, E1, S["patches1"], S["patchT1"])),
                (4, a_norm3_T), (3, a_norms_T), (4, a_hid1), (0, a_h0), (3, a_tanh_hid), (3, a_qk1),
                (0, a_norm0T), (3, a_tanh_par), (0, a_v(0)), (0, a_v(1)), (4, a_store), (3, a_interference), (1, a_exp),
                (0, a_qk(0)), (2, a_int_in), (2, a_in_T), (0, a_qk(1)), (2, a_tanh_gate), (0, a_qk(2)),
                (1, a_probsT[0]), (1, a_probsT[1]), (1, a_probsT[2]), (2, a_square), (1, a_att[0]), (1, a_att[1]),
                (2, a_int_out), (2, a_out_T), (3, a_att1_T),
            ]))
            act.wait_ge(stored[0], 16 * ((GROUPS + 1) // 2))
            act.wait_ge(stored[1], 16 * (GROUPS // 2))

        @block.tensor
        def _(pe):
            def turn(dst, src, identity):
                return pe.transpose(dst, src, identity)

            pe.wait_ge(ld_const, 16)
            pe.wait_ge(ld_tok, 48)
            for k in range(0, CHUNKS, 2):
                if k == 4:
                    pe.wait_ge(setup_act, 1)
                for j in range(2):
                    for e in range(2):
                        last = turn((E0 if k % 4 == 0 else E1)[:, j * EMBED + e * HALF:j * EMBED + (e + 1) * HALF],
                                    w_tok_raw[:, e, (k + j) * 128:(k + j + 1) * 128], ident[0:HALF, 0:HALF])
                last.then_inc(setup_turned, 1)
            pe.wait_ge(ld_lin, 16 * 25)
            for k in range(2):
                last = turn(L0[0:HALF, k * HIDDEN1:(k + 1) * HIDDEN1], w1_raw[:, k * HALF:(k + 1) * HALF], ident)
            last.then_inc(setup_turned, 1)
            for k in range(2):
                for e in range(2):
                    last = turn(L1[0:HALF, k * EMBED + e * HALF:k * EMBED + (e + 1) * HALF],
                                wo_raw[:, e, k * HALF:(k + 1) * HALF], ident[0:HALF, 0:HALF])
            last.then_inc(setup_turned, 1)
            pe.wait_ge(setup_pool, 1)
            pe.wait_ge(setup_sums, 1)
            pe.matmul(M0[:, 0:2], ones[:, :], abs_sums[:, :], start=True, stop=True).then_inc(setup_pe, 1)
            pe.wait_ge(setup_ternary, 1)
            for n in range(4):
                if n >= 2:
                    pe.wait_ge(setup_act, 3 + 2 + n - 1)
                for k in range(2):
                    for j in range(2):
                        last = turn((A0, A1)[n % 2][:, :].bitcast(BF16)[0:HALF, k * 256 + j * 128:k * 256 + (j + 1) * 128],
                                    w_in_q[:, 2 * n + j, k * HALF:(k + 1) * HALF], ident_b[:, :])
                last.then_inc(setup_turned, 1)
            for n in range(2):
                pe.wait_ge(setup_act, 3 + 2 + 3 + n)
                for k in range(2):
                    for e in range(2):
                        last = turn((A0, A1)[n % 2][:, :].bitcast(BF16)[:, k * EMBED + e * HALF:k * EMBED + (e + 1) * HALF],
                                    w_out_q[:, e, (2 * n + k) * 128:(2 * n + k + 1) * 128], ident_b[0:HALF, 0:HALF])
                last.then_inc(setup_turned, 1)
            pe.wait_ge(setup_act, 3 + 2)
            for bank_tile, c0, c1 in ((L0, 0, 384), (L1, 384, 576)):
                for k in range(2):
                    pe.matmul(bank_tile[0:1, 0:c1 - c0], ln_wb[:, k, 1:2], w_qkv1_raw[:, k, c0:c1], start=k == 0, stop=k == 1)
            for k in range(2):
                last = pe.matmul(L1[0:1, 192:384], mn_wb[:, 1:2], w_p1_raw[:, k, :], start=k == 0, stop=k == 1)
            last.then_inc(setup_pe, 1)
            pe.wait_ge(setup_act, 3 + 2 + 4 + 2)
            for k in range(2):
                pe.matmul(A1[:, 0:EMBED], w2_raw[:, k, :], wo[:, k, :], start=k == 0, stop=k == 1)
            for k in range(2):
                last = pe.matmul(A1[0:1, EMBED:2 * EMBED], b2_col[:, k:k + 1], wo[:, k, :], start=k == 0, stop=k == 1)
            last.then_inc(setup_pe, 1)
            pe.wait_ge(ready, READY)
            pe.wait_ge(ld_qkv, 32)
            pe.wait_ge(ld_late, 16 * 10)

            def t_patches(n, bank_tile, freed, done_sem):
                def step(g, p):
                    pe.wait_ge(S["strips_cut"], g + 1)
                    after(pe, freed, g)
                    dst = bank_tile[:, 0:STRIPS * GRID].rearrange("p (s x) -> p s x", x=GRID)
                    for x in range(GRID):
                        last = turn(dst[:, :, x], patches[:, x, 128 * n:128 * (n + 1)], ident[0:STRIPS, 0:STRIPS])
                    last.then_inc(done_sem, 1)
                return step

            def t_embed(g, p):
                pe.wait_ge(S["patchT0"], g + 1)
                pe.wait_ge(S["patchT1"], g + 1)
                for k in range(CHUNKS):
                    pe.matmul(E0[0:ROWS, 0:EMBED], patchT[:, k, :], w_tok[:, k, :], start=k == 0, stop=False)
                pe.matmul(E0[0:ROWS, 0:EMBED], token_kind, start_rows[:, :], start=False, stop=True).then_inc(S["embedded"], 1)

            def t_norm0(g, p):
                pe.wait_ge(S["norm0"], g + 1)
                for k in range(2):
                    last = turn(parts(E1, 2)[0:HALF, k], norm0[:, k * HALF:(k + 1) * HALF], ident[0:ROWS, 0:ROWS])
                last.then_inc(S["norm0_turned"], 1)

            def t_v(n):
                def step(g, p):
                    pe.wait_ge(S["norm0T"], g + 1)
                    if n == 0:
                        pe.wait_ge(S["h0_copied"], g + 1)
                    for k in range(2):
                        last = pe.matmul((E0, E1)[n][0:ROWS, 0:384], norm0T[:, k, :],
                                         w_qkv0[:, k, 2 * INNER + n * 384:2 * INNER + (n + 1) * 384], start=k == 0, stop=k == 1)
                    last.then_inc((S["v_half0"], S["v_half1"])[n], 1)
                return step

            def t_qk(n):
                def step(g, p):
                    pe.wait_ge((S["v_copied0"], S["v_copied1"], S["qk_copied0"])[n], g + 1)
                    for j in range(4):
                        for k in range(2):
                            tile = 4 * n + j
                            last = pe.matmul(parts((E0, E1, E0)[n], 4)[:, j], w_qkv0[:, k, tile * 128:(tile + 1) * 128],
                                             norm0T[:, k, :], start=k == 0, stop=k == 1)
                    last.then_inc((S["qk_done0"], S["qk_done1"], S["qk_done2"])[n], 1)
                return step

            def t_dots(f):
                def step(g, p):
                    if f == 0:
                        pe.wait_ge(S["qk_copied2"], g + 1)
                    if f == 0:
                        after(pe, S["att_copied1"], g)
                    elif f == 1:
                        after(pe, S["h1"], g)
                    else:
                        pe.wait_ge((S["packed0"], S["packed1"])[f - 2], g + 1)
                    dst = parts((A0, A1)[f % 2], 3)[0:ROWS]
                    pe.matmul(dst, ident_b[0:ROWS, 0:ROWS], score_mask_b[:, :].unsqueeze(1).to_broadcast([ROWS, 3, ROWS]),
                              start=True, stop=False, skip_group_check=True)
                    r = HEAD0 * (f // 2)
                    for j in range(3):
                        tile = 3 * (f % 2) + j
                        last = pe.matmul(dst[:, j], qkT[r:r + HEAD0, p, tile, :], qkT[r:r + HEAD0, p, QTILES + tile, :],
                                         start=False, stop=j == 2, skip_group_check=True)
                    last.then_inc((S["dots0"], S["dots1"], S["dots2"], S["dots3"])[f], 1)
                return step

            def t_probs(f):
                def step(g, p):
                    pe.wait_ge((S["widened0"], S["widened1"], S["widened2"])[f], g + 1)
                    if f == 2:
                        pe.wait_ge(S["probsT0"], g + 1)
                    for j in range(4):
                        last = turn(parts((A0, A1, A0)[f], 4)[0:ROWS, j], wide[:, 4 * f + j].rearrange("p b j -> p (b j)"),
                                    ident[0:ROWS, 0:ROWS])
                    last.then_inc((S["turned0"], S["turned1"], S["turned2"])[f], 1)
                return step

            def t_att0(n):
                def step(g, p):
                    pe.wait_ge(S["probsT2"], g + 1)
                    if n == 0:
                        pe.wait_ge(S["v_copied1"], g + 1)
                    dst = parts((A1, A0)[n], 3)
                    for odd in range(2):
                        for j in range(3):
                            tile = 3 * n + j
                            head = 2 * tile + odd
                            last = pe.matmul(dst[64 * odd:64 * odd + 64, j], v0[:, p, head * HEAD0:(head + 1) * HEAD0],
                                             probsT[:, QTILES * odd + tile, :], start=True, stop=True)
                    last.then_inc((S["att_done0"], S["att_done1"])[n], 1)
                return step

            def t_proj0(g, p):
                pe.wait_ge(S["att_copied0"], g + 1)
                pe.matmul(A1[0:ROWS, 0:EMBED], ones[0:1, 0:ROWS], b_o0[:, :], start=True, stop=False)
                for t in range(QTILES):
                    if t == 3:
                        pe.wait_ge(S["att_copied1"], g + 1)
                    last = pe.matmul(A1[0:ROWS, 0:EMBED], att0T[:, t, :], w_o0[:, t, :], start=False, stop=t == QTILES - 1)
                last.then_inc(S["proj0"], 1)

            def t_int_in(g, p):
                pe.wait_ge(S["int_in"], g + 1)
                after(pe, S["hid1_copied"], g - 1)
                after(pe, S["h2"], g)
                for k in range(2):
                    last = turn(M0[:, :].bitcast(BF16)[0:HALF, k * 128:k * 128 + ROWS],
                                int_in[:, k * HALF:(k + 1) * HALF], ident_b[0:ROWS, 0:ROWS])
                last.then_inc(S["in_turned"], 1)

            def t_gate(g, p):
                pe.wait_ge(S["in_copied"], g + 1)
                after(pe, S["scaled4"], g - 1)
                for k in range(2):
                    last = pe.matmul(M1[0:ROWS, :], int_inT[:, k, :], w_in[:, k, HIDDEN0:2 * HIDDEN0], start=k == 0, stop=k == 1)
                last.then_inc(S["gate_done"], 1)
                for k in range(2):
                    last = pe.matmul(M0[0:ROWS, :], int_inT[:, k, :], w_in[:, k, 0:HIDDEN0], start=k == 0, stop=k == 1)
                last.then_inc(S["up_done"], 1)

            def t_int_out(g, p):
                pe.wait_ge(S["int_out"], g + 1)
                for k in range(4):
                    last = turn(M1[:, :].bitcast(BF16)[:, k * 128:k * 128 + ROWS],
                                int_out[:, k * 128:(k + 1) * 128], ident_b[0:ROWS, 0:ROWS])
                last.then_inc(S["out_turned"], 1)

            def t_down(g, p):
                pe.wait_ge(S["out_copied"], g + 1)
                for k in range(4):
                    last = pe.matmul(M0[0:ROWS, 0:EMBED], int_outT[:, k, :], w_out[:, k, :], start=k == 0, stop=k == 3)
                last.then_inc(S["down_done"], 1)

            def t_norms2(g, p):
                pe.wait_ge(S["norms2"], g + 1)
                after(pe, S["h3"], g)
                for n in range(2):
                    for k in range(2):
                        last = turn(parts(L0, 4)[0:HALF, 2 * n + k], norms2[:, n, k * HALF:(k + 1) * HALF],
                                    ident[0:ROWS, 0:ROWS])
                last.then_inc(S["norms_turned"], 1)

            def t_lin_in(g, p):
                pe.wait_ge(S["norms_copied"], g + 1)
                for k in range(2):
                    rows = HALF + 1 - k
                    pe.matmul(L0[0:ROWS, 128:128 + EMBED], norms2T[0:rows, 2 + k, :],
                              w_qkv1[0:rows, k, 2 * EMBED:3 * EMBED], start=k == 0, stop=k == 1)
                for k in range(2):
                    last = pe.matmul(L0[:, 0:ROWS], w_g1[:, k, :], norms2T[0:HALF, k, :], start=k == 0, stop=k == 1)
                last.then_inc(S["hid"], 1)
                for j in range(4):
                    for k in range(2):
                        rows = HALF + 1 - k
                        last = pe.matmul(parts(L1, 4)[0:HALF, j], w_qkv1[0:rows, k, j * HALF:(j + 1) * HALF],
                                         norms2T[0:rows, 2 + k, :], start=k == 0, stop=k == 1)
                last.then_inc(S["qk1"], 1)

            def t_params(g, p):
                pe.wait_ge(S["hidT"], g + 1)
                pe.matmul(L0[0:ROWS, 384:384 + HEADS * GATES], hidT[:, :], w_g2[:, :, :].rearrange("p h n -> p (h n)"),
                          start=True, stop=True).then_inc(S["params"], 1)

            def t_lin(q):
                def step(g, p):
                    if q == 0:
                        pe.wait_ge(S["feat_q"], g + 1)
                        pe.wait_ge(S["feat_k"], g + 1)
                    if q == 1:
                        pe.wait_ge(S["v1"], g + 1)
                    if q == 2:
                        pe.wait_ge(S["a_masked0"], g + 1)
                    for t in range(2):
                        for odd in range(2):
                            last = pe.matmul(parts((L1, L0, L1)[q], 4)[0:ROWS, 2 * t + odd],
                                             feat_k[32 * q:32 * q + 32, odd, t, :], feat_qk[32 * q:32 * q + 32, t, :],
                                             start=True, stop=True)
                    last.then_inc((S["a_done0"], S["a_done1"], S["a_done2"])[q], 1)
                return step

            def t_num(g, p):
                pe.wait_ge(S["a_masked1"], g + 1)
                pe.wait_ge(S["a_masked2"], g + 1)
                pe.wait_ge(S["a_masked0"], g + 1)
                pe.wait_ge(S["v1"], g + 1)
                for q in range(3):
                    for t in range(2):
                        for odd in range(2):
                            head = 6 * t + 2 * q + odd
                            last = pe.matmul(L0[0:ROWS, head * (HEAD1 + 1):(head + 1) * (HEAD1 + 1)],
                                             weightsT[:, 4 * q + 2 * t + odd, :], v1[:, head, :], start=True, stop=True)
                last.then_inc(S["num"], 1)

            def t_att1(g, p):
                pe.wait_ge(S["att1"], g + 1)
                flat = att1[:, :, :].rearrange("p h d -> p (h d)")
                for k in range(2):
                    last = turn(parts(L1, 2)[0:HALF, k], flat[:, k * HALF:(k + 1) * HALF], ident[0:ROWS, 0:ROWS])
                last.then_inc(S["att1_turned"], 1)

            def t_proj1(g, p):
                pe.wait_ge(S["att1_copied"], g + 1)
                for k in range(2):
                    rows = HALF + 1 - k
                    last = pe.matmul(L0[0:ROWS, 256:256 + EMBED], att1T[0:rows, k, :], w_p1[0:rows, k, :],
                                     start=k == 0, stop=k == 1)
                last.then_inc(S["proj1"], 1)

            def of_stage2(count):
                return min(count, GROUPS) if isinstance(count, int) else count

            def t_norm3(g, p):
                pe.wait_ge(S["norm3"], g + 1)
                after(pe, S["scaled4"], g)
                pe.wait_ge(S["out_copied"], of_stage2(g + 2))
                for k in range(2):
                    last = turn(parts(M1, 2)[0:HALF, k], norm3[:, k * HALF:(k + 1) * HALF], ident[0:ROWS, 0:ROWS])
                last.then_inc(S["norm3_turned"], 1)

            def t_hid1(g, p):
                pe.wait_ge(S["norm3_copied"], g + 1)
                pe.wait_ge(S["h2"], of_stage2(g + 2))
                for k in range(2):
                    rows = HALF + 1 - k
                    last = pe.matmul(M0[:, 0:ROWS], w1[0:rows, k, :], norm3T[0:rows, k, :], start=k == 0, stop=k == 1)
                last.then_inc(S["hid1"], 1)

            def t_out4(g, p):
                pe.wait_ge(S["hid1_copied"], g + 1)
                pe.matmul(M1[0:ROWS, 0:EMBED], ones[0:1, 0:ROWS], b2o[:, :], start=True, stop=False)
                pe.matmul(M1[0:ROWS, 0:EMBED], hid1T[:, :], w2o[:, :], start=False, stop=True).then_inc(S["out4"], 1)

            iterations(pe, lambda i, parity, active: in_turn(i, parity, active, [
                (1, t_dots(0)), (1, t_dots(1)), (0, t_patches(0, E0, S["qk_copied2"], S["patches0"])),
                (0, t_patches(1, E1, S["qk_copied1"], S["patches1"])), (4, t_norm3), (3, t_norms2), (1, t_dots(2)), (1, t_dots(3)),
                (0, t_embed), (4, t_hid1), (3, t_lin_in), (4, t_out4), (0, t_norm0), (3, t_params),
                (0, t_v(0)), (0, t_v(1)), (0, t_qk(0)), (3, t_lin(0)), (2, t_int_in), (0, t_qk(1)), (2, t_gate),
                (3, t_lin(1)), (0, t_qk(2)), (1, t_probs(0)), (1, t_probs(1)), (3, t_lin(2)), (1, t_probs(2)), (3, t_num),
                (1, t_att0(0)), (1, t_att0(1)), (2, t_int_out), (3, t_att1), (1, t_proj0), (2, t_down), (3, t_proj1),
            ]))


def kernel(**inputs):
    import concourse.bacc as bacc
    from concourse.bass_utils import run_bass_kernel_spmd

    nc = bacc.Bacc("TRN2", target_bir_lowering=False, num_devices=1)
    arrays, handles = {}, {}
    for name, value in inputs.items():
        arrays[name] = np.ascontiguousarray(value)
        handles[name] = nc.dram_tensor(name, arrays[name].shape, F32, kind="ExternalInput").ap()
    arrays["constants"] = constant_table()
    table = nc.dram_tensor("constants", arrays["constants"].shape, F32, kind="ExternalInput").ap()
    out = nc.dram_tensor("out", (IMAGES, TOKENS, EMBED), F32, kind="ExternalOutput").ap()
    build(nc, handles, table, out.rearrange("b t n -> (b t) n"))
    return run_bass_kernel_spmd(nc, [arrays], core_ids=[0]).results[0]["out"]
```

```python
from contextlib import ExitStack

import numpy as np

import concourse.bass as bass
from concourse import mybir

F32 = mybir.dt.float32
BF16 = mybir.dt.bfloat16
ALU = mybir.AluOpType
ACT = mybir.ActivationFunctionType
X = mybir.AxisListType.X

IMAGES, CHANNELS, SIDE = 128, 3, 64
PATCH = 16
GRID = SIDE // PATCH
TOKENS = GRID * GRID + 1
EMBED = 192
PER = 7
ROWS = PER * TOKENS
GROUPS = -(-IMAGES // PER)
LAST_IMAGE = IMAGES - PER
STRIPS = PER * CHANNELS * GRID
CHUNKS = CHANNELS * PATCH * PATCH // 128
HALF = EMBED // 2
HEADS = 12
HEAD0 = 64
INNER = HEADS * HEAD0
QTILES = INNER // 128
KEEP = int(TOKENS * 0.75)
DROP = TOKENS - 1 - KEEP
HIDDEN0 = 512
HEAD1 = EMBED // HEADS
HIDDEN1 = 128
SLOT = 32
NUM_TILES = HEADS * SLOT // 128
GATES = 5
SINE_ORDER = 6
DEPTH = 6
STEPS = GROUPS + DEPTH - 1

BIG = float(2.0 ** 100)
FILLER = -float(2.0 ** 110)
ROUND = 1.5 * 2.0 ** 23
EPS = 1e-5
EPS_RMS = 1e-6
EPS_QUANT = 1e-5
EPS_DEN = 1e-6

C_IDENT, C_SCORE, C_BLOCK, C_CAUSAL, C_KIND, C_PARITY = 0, 128, 256, 384, 512, 640
C_WIDTH = 642


def constant_table():
    t = np.zeros((128, C_WIDTH), np.float32)
    image = np.arange(ROWS) // TOKENS
    same = image[:, None] == image[None, :]
    t[:, C_IDENT:C_IDENT + 128] = np.eye(128)
    t[:ROWS, C_SCORE:C_SCORE + ROWS] = np.where(same, np.where(np.eye(ROWS, dtype=bool), BIG, 0.0), -BIG)
    t[:ROWS, C_BLOCK:C_BLOCK + ROWS] = same
    t[:ROWS, C_CAUSAL:C_CAUSAL + ROWS] = same & (np.arange(ROWS)[:, None] <= np.arange(ROWS)[None, :])
    t[0, C_KIND:C_KIND + ROWS] = np.arange(ROWS) % TOKENS > 0
    t[1, C_KIND:C_KIND + ROWS] = np.arange(ROWS) % TOKENS == 0
    t[:, C_PARITY] = np.arange(128) % 32 < HEAD1
    t[:, C_PARITY + 1] = np.arange(128) % 32 >= HEAD1
    return t


def sine_coefficients():
    w = np.sqrt((np.cos(np.pi * (np.arange(64) + 0.5) / 64) + 1) / 2)
    c = np.polyfit(w * w, np.sqrt(2) * np.sin(np.pi * w) / (2 * w), SINE_ORDER)
    return [float(x / 4.0 ** (SINE_ORDER - n)) for n, x in enumerate(c)]


def build(nc, a, table, out):
    ctx = ExitStack()
    with ctx:
        def sb(name, shape, dt=F32):
            return ctx.enter_context(nc.sbuf_tensor(name, shape, dt))

        def sem(name):
            return ctx.enter_context(nc.semaphore(name))

        consts = sb("consts", [128, C_WIDTH])
        ident = consts[:, C_IDENT:C_IDENT + 128]
        block_mask = consts[0:ROWS, C_BLOCK:C_BLOCK + ROWS]
        causal_mask = consts[0:ROWS, C_CAUSAL:C_CAUSAL + ROWS]
        token_kind = consts[0:2, C_KIND:C_KIND + ROWS]
        ident_b = sb("ident_b", [128, 128], BF16)
        score_mask_b = sb("score_mask_b", [ROWS, ROWS], BF16)
        ones = sb("ones", [128, 128])
        minus_half = sb("minus_half", [128, HEADS])
        gain_eps = sb("gain_eps", [128, 8])
        eps_head = sb("eps_head", [128, HEADS])
        sine_terms = sb("sine_terms", [128, SINE_ORDER + 1, HEADS])

        w_tok_raw = sb("w_tok_raw", [HALF, 2, CHUNKS * 128])
        w_tok = sb("w_tok", [128, CHUNKS, EMBED])
        start_rows = sb("start_rows", [2, EMBED])
        start = sb("start", [ROWS, EMBED])
        w_qkv0 = sb("w_qkv0", [HALF, 2, 3 * INNER])
        scale_b = sb("scale_b", [HALF, HEADS])
        w_o0 = sb("w_o0", [128, QTILES, EMBED])
        b_o0 = sb("b_o0", [ROWS, EMBED])
        w_in_raw = sb("w_in_raw", [128, 2 * HIDDEN0 // 128, EMBED])
        w_in_q = sb("w_in_q", [128, 2 * HIDDEN0 // 128, EMBED], BF16)
        w_in = sb("w_in", [HALF, 2, 2 * HIDDEN0], BF16)
        g_in = sb("g_in", [ROWS, EMBED])
        w_out_raw = sb("w_out_raw", [HALF, 2, HIDDEN0])
        w_out_q = sb("w_out_q", [HALF, 2, HIDDEN0], BF16)
        w_out = sb("w_out", [128, HIDDEN0 // 128, EMBED], BF16)
        g_out = sb("g_out", [ROWS, HIDDEN0])
        abs_sums = sb("abs_sums", [128, 2])
        w_scale = sb("w_scale", [128, 2])
        w_scale_inv = sb("w_scale_inv", [128, 2])
        w_scale_127 = sb("w_scale_127", [128, 2])
        w_qkv1 = sb("w_qkv1", [HALF + 1, 2, 3 * EMBED])
        w_qkv1_raw = sb("w_qkv1_raw", [HALF, 2, 3 * EMBED])
        ln_wb = sb("ln_wb", [HALF, 2, 2])
        b_qkv1 = sb("b_qkv1", [1, 3 * EMBED])
        w_g1 = sb("w_g1", [HALF, 2, HIDDEN1])
        w_g2 = sb("w_g2", [HIDDEN1, HEADS, GATES])
        temp = sb("temp", [ROWS, 1])
        w_p1_raw = sb("w_p1_raw", [HALF, 2, EMBED])
        w_p1 = sb("w_p1", [HALF + 1, 2, EMBED])
        b_p1 = sb("b_p1", [1, EMBED])
        mn_wb = sb("mn_wb", [HALF, 2])
        w1_raw = sb("w1_raw", [HIDDEN1, EMBED])
        w1 = sb("w1", [HALF + 1, 2, HIDDEN1])
        w2_raw = sb("w2_raw", [HALF, 2, HIDDEN1])
        wo_raw = sb("wo_raw", [HALF, 2, EMBED])
        wo = sb("wo", [HALF, 2, EMBED])
        b2_col = sb("b2_col", [HALF, 2])
        w2o = sb("w2o", [HIDDEN1, EMBED])
        b2o_row = sb("b2o_row", [1, EMBED])
        b2o = sb("b2o", [ROWS, EMBED])
        bo = sb("bo", [1, EMBED])
        gamma = sb("gamma", [ROWS, EMBED])
        beta = sb("beta", [ROWS, EMBED])

        strips = sb("strips", [STRIPS, 2, PATCH, SIDE])
        patches = sb("patches", [STRIPS, GRID, PATCH * PATCH])
        patchT = sb("patchT", [128, CHUNKS, ROWS])
        h0 = sb("h0", [ROWS, 2, EMBED])
        stats0 = sb("stats0", [ROWS, 6])
        moments0 = sb("moments0", [ROWS, 2])
        spread0 = sb("spread0", [ROWS, 1])
        rstd0 = sb("rstd0", [ROWS, 1])
        norm0 = sb("norm0", [ROWS, EMBED])
        norm0T = sb("norm0T", [HALF, 2, ROWS])
        qkT = sb("qkT", [128, 2, 2 * QTILES, ROWS])
        v0 = sb("v0", [ROWS, 2, INNER])

        ROWLEN = TOKENS + 8 - DROP - 1
        scores = sb("scores", [ROWS, HEADS, ROWLEN])
        score_sum = sb("score_sum", [ROWS, TOKENS])
        top = sb("top", [ROWS, HEADS, 8])
        kept = sb("kept", [ROWS, HEADS, ROWLEN])
        mixed = sb("mixed", [ROWS, HEADS, TOKENS])
        least = sb("least", [ROWS, HEADS])
        shifted = sb("shifted", [ROWS, HEADS, TOKENS])
        expd = sb("expd", [ROWS, HEADS, TOKENS])
        exp_sum = sb("exp_sum", [ROWS, HEADS])
        exp_inv = sb("exp_inv", [ROWS, HEADS])
        probs = sb("probs", [ROWS, HEADS, TOKENS])
        wide = sb("wide", [ROWS, HEADS, PER, TOKENS])
        probsT = sb("probsT", [ROWS, HEADS, ROWS])
        att0T = sb("att0T", [128, QTILES, ROWS])
        h1 = sb("h1", [ROWS, 2, EMBED])

        stats1 = sb("stats1", [ROWS, 6])
        moments1 = sb("moments1", [ROWS, 2])
        spread1 = sb("spread1", [ROWS, 2])
        rstd1 = sb("rstd1", [ROWS, 1])
        u_in = sb("u_in", [ROWS, EMBED])
        umax_in = sb("umax_in", [ROWS, 1])
        amax_in = sb("amax_in", [ROWS, 1])
        ainv_in = sb("ainv_in", [ROWS, 1])
        quant_in = sb("quant_in", [ROWS, 1])
        unit_in = sb("unit_in", [ROWS, 2])
        big_in = sb("big_in", [ROWS, EMBED])
        int_in = sb("int_in", [ROWS, EMBED], BF16)
        int_inT = sb("int_inT", [HALF, 2, ROWS], BF16)
        tanh_gate = sb("tanh_gate", [ROWS, HIDDEN0])
        gated = sb("gated", [ROWS, HIDDEN0])
        product = sb("product", [ROWS, HIDDEN0])
        scaled = sb("scaled", [ROWS, HIDDEN0])
        squares = sb("squares", [ROWS, HIDDEN0])
        half_c2 = sb("half_c2", [ROWS, 2])
        square_sum = sb("square_sum", [ROWS, 1])
        mean_square = sb("mean_square", [ROWS, 1])
        rms_inv = sb("rms_inv", [ROWS, 1])
        row_gain = sb("row_gain", [ROWS, 1])
        umax_out = sb("umax_out", [ROWS, 1])
        amax_out = sb("amax_out", [ROWS, 1])
        ainv_out = sb("ainv_out", [ROWS, 1])
        quant_out = sb("quant_out", [ROWS, 1])
        unit_out = sb("unit_out", [ROWS, 1])
        big_out = sb("big_out", [ROWS, HIDDEN0])
        int_out = sb("int_out", [ROWS, HIDDEN0], BF16)
        int_outT = sb("int_outT", [128, HIDDEN0 // 128, ROWS], BF16)
        h2 = sb("h2", [ROWS, 2, EMBED])

        stats2 = sb("stats2", [ROWS, 6])
        moments2 = sb("moments2", [ROWS, 2])
        spread2 = sb("spread2", [ROWS, 2, 2])
        rstd2 = sb("rstd2", [ROWS, 2])
        norms2 = sb("norms2", [ROWS, 2, EMBED])
        norms2T = sb("norms2T", [HALF + 1, 4, ROWS])
        exp_qk = sb("exp_qk", [HALF, 4, ROWS])
        relu_qk = sb("relu_qk", [HALF, 4, ROWS])
        feat_qk = sb("feat_qk", [HALF, 4, ROWS])
        feat_k = sb("feat_k", [HALF, 2, 2, ROWS])
        tanh_hid = sb("tanh_hid", [HIDDEN1, ROWS])
        hidT = sb("hidT", [HIDDEN1, ROWS])
        tanh_par = sb("tanh_par", [ROWS, HEADS, GATES])
        wave = sb("wave", [ROWS, HEADS])
        wave_sq = sb("wave_sq", [ROWS, HEADS])
        poly = sb("poly", [ROWS, 2, HEADS])
        amp = sb("amp", [ROWS, 2, HEADS])
        amps = sb("amps", [ROWS, HEADS])
        sine = sb("sine", [ROWS, HEADS])
        sine_sq = sb("sine_sq", [ROWS, HEADS])
        cosine = sb("cosine", [ROWS, HEADS])
        overlap = sb("overlap", [ROWS, HEADS])
        tanh_over = sb("tanh_over", [ROWS, HEADS])
        tanh_int = sb("tanh_int", [ROWS, HEADS])
        v_raw = sb("v_raw", [ROWS, HEADS, HEAD1])
        v1 = sb("v1", [ROWS, HEADS, SLOT])
        weightsT = sb("weightsT", [ROWS, HEADS, ROWS])
        numT = sb("numT", [128, NUM_TILES, ROWS])
        den = sb("den", [ROWS, HEADS])
        den_inv = sb("den_inv", [ROWS, HEADS])
        ratio = sb("ratio", [ROWS, HEADS, HEAD1])
        ratio_sum = sb("ratio_sum", [ROWS, HEADS])
        centred = sb("centred", [ROWS, HEADS, HEAD1])
        centred_sq = sb("centred_sq", [ROWS, HEADS, HEAD1])
        sq_sum = sb("sq_sum", [ROWS, HEADS])
        spread_h = sb("spread_h", [ROWS, HEADS])
        rstd_h = sb("rstd_h", [ROWS, HEADS])
        att1 = sb("att1", [ROWS, HEADS, HEAD1])
        att1T = sb("att1T", [HALF + 1, 2, ROWS])
        h3 = sb("h3", [ROWS, 2, EMBED])

        stats3 = sb("stats3", [ROWS, 6])
        moments3 = sb("moments3", [ROWS, 2])
        spread3 = sb("spread3", [ROWS, 1])
        rstd3 = sb("rstd3", [ROWS, 1])
        norm3 = sb("norm3", [ROWS, EMBED])
        norm3T = sb("norm3T", [HALF + 1, 2, ROWS])
        hid1T = sb("hid1T", [HIDDEN1, ROWS])
        h3_beta = sb("h3_beta", [ROWS, EMBED])
        stats4 = sb("stats4", [ROWS, 6])
        moments4 = sb("moments4", [ROWS, 2])
        spread4 = sb("spread4", [ROWS, 1])
        rstd4 = sb("rstd4", [ROWS, 1])
        out4 = sb("out4", [ROWS, EMBED])
        scaled4 = sb("scaled4", [ROWS, EMBED])
        result = sb("result", [ROWS, 2, EMBED])
        pad_pool = sb("pad_pool", [128, 1])
        pad_act = sb("pad_act", [128, 1])
        pad_drop = sb("pad_drop", [128, 1])
        pad = sb("pad", [128, 1])

        bank = {n: [ctx.enter_context(nc.psum_tensor(f"bank_{n}{i}", [128, 512], F32)) for i in range(2)]
                for n in ("embed", "att", "ffn", "lin")}
        E0, E1 = bank["embed"]
        A0, A1 = bank["att"]
        M0, M1 = bank["ffn"]
        L0, L1 = bank["lin"]

        step_names = """
            strips_cut patches0 patches1 patchT0 patchT1 embedded h0_copied h0_biased stats0 moments0 spread0 rstd0
            norm0 norm0_turned norm0T v_half0 v_half1 v_copied0 v_copied1
            qk_done0 qk_done1 qk_done2 qk_copied0 qk_copied1 qk_copied2
            dots01 dots23 packed0 packed1 packed2 packed3 shifted expd probs
            widened0 widened1 widened2 turned0 turned1 turned2 probsT0 probsT1 probsT2 att_done0 att_done1 att_copied0 att_copied1
            proj0 h1
            moments1 rstd1 unit_in half_c2 big_in int_in in_turned in_copied gate_done up_done tanh_gate
            product scaled square_sum mean_square rms_inv big_out int_out out_turned out_copied down_done h2
            stats2 moments2 rstd2 norms2 norms_turned norms_copied qk1 hid relu_qk feat_q feat_k_all feat_k
            tanh_hid hidT params tanh_par overlap tanh_over tanh_int v1
            a_done01 a_done2 a_masked0 a_masked1 a_masked2 num_done num_copied num centred centred_sq sq_sum rstd_h
            att1 att1_turned att1_copied proj1 h3
            moments3 rstd3 norm3 norm3_turned norm3_copied hid1 hid1_copied h3_beta out4 out4_copied
            moments4 rstd4 scaled4 result
        """.split()
        S = {n: sem("s_" + n) for n in step_names}
        RUN = {n: sem("run_" + n) for n in "v_att v_in v_out v_lin v_last p_ffn p_lin p_gate p_head p_last".split()}
        strips_in = [sem("strips_in0"), sem("strips_in1")]
        stored = [sem("stored0"), sem("stored1")]
        ld_const, ld_tok, ld_qkv, ld_ffn, ld_lin, ld_att, ld_late, ld_bias = (
            sem("ld_" + n) for n in ("const", "tok", "qkv", "ffn", "lin", "att", "late", "bias"))
        setup_pe, setup_turned, setup_dve, setup_sums, setup_ternary, setup_act, setup_pool, setup_row = (
            sem("setup_" + n) for n in ("pe", "turned", "dve", "sums", "ternary", "act", "pool", "row"))
        ready = sem("ready")
        READY_FIRST, READY = 1, 3

        def late_setup(eng):
            eng.wait_ge(ready, READY)
            eng.wait_ge(ld_late, 16 * 6)
        block = ctx.enter_context(nc.Block())

        def after(eng, semaphore, count):
            if not isinstance(count, int) or count > 0:
                eng.wait_ge(semaphore, count)

        def chain_of(eng, semaphore, links):
            count = [0]

            def then(g, instruction):
                count[0] = count[0] % links + 1
                instruction.then_inc(semaphore, 1)
                eng.wait_ge(semaphore, g * links + count[0])
            return then

        def iterations(eng, run, setup):
            first = DEPTH + 1 + (DEPTH + 1) % 2
            end = first + (GROUPS - first) // 2 * 2
            for i in range(first):
                run(i, i % 2, [0 <= i - n < GROUPS for n in range(DEPTH)])
                if i < len(setup):
                    setup[i]()
            with eng.Fori(0, (end - first) // 2) as pair:
                run(2 * pair + first, 0, [True] * DEPTH)
                run(2 * pair + (first + 1), 1, [True] * DEPTH)
            for i in range(end, STEPS):
                run(i, i % 2, [0 <= i - n < GROUPS for n in range(DEPTH)])

        def in_turn(i, parity, active, steps):
            for behind, step in steps:
                if active[behind]:
                    step(i - behind, (parity + behind) % 2)

        def row(ap):
            return ap.rearrange("(o n) -> o n", o=1)

        def parts(tile, n):
            return tile[:, 0:n * ROWS].rearrange("p (n r) -> p n r", n=n)

        @block.sync
        def _(sp):
            all_strips = a["x"].rearrange("b c (y r) w -> (b c y) (r w)", r=PATCH)

            def load(semaphore, dst, src):
                sp.dma_start(dst, src).then_inc(semaphore, 16)

            def load_column(semaphore, dst, src):
                sp.dma_start(dst, src, allow_slow_non_contiguous=True).then_inc(semaphore, 16)

            def load_strips(g, p):
                after(sp, S["strips_cut"], g - 1)
                first = g * PER if not isinstance(g, int) else min(g * PER, LAST_IMAGE)
                sp.dma_start(strips[:, p].rearrange("s r w -> s (r w)"),
                             all_strips[bass.ds(first * CHANNELS * GRID, STRIPS), :]).then_inc(strips_in[p], 16)

            load(ld_const, consts[:, :], table)
            load(ld_tok, w_tok_raw[:, :, :], a["L0_tok_W"].rearrange("(k p) n -> p k n", k=2))
            load(ld_tok, start_rows[0:1, :], row(a["L0_tok_b"]))
            load(ld_tok, start_rows[1:2, :], a["cls_tok"].rearrange("a b n -> (a b) n"))
            load_strips(0, 0)
            load(ld_bias, b_o0[:, :], a["L0_attn_b_out"].partition_broadcast(ROWS))
            load(ld_qkv, w_qkv0[:, :, :], a["L0_attn_w_qkv"].rearrange("(k p) n -> p k n", k=2))
            load(ld_qkv, scale_b[:, :], a["L0_attn_scale"].partition_broadcast(HALF))
            load_strips(1, 1)
            load(ld_ffn, w_in_raw[:, :, :], a["L0_ffn_w_in"].rearrange("(k p) n -> p k n", p=128))
            load(ld_ffn, w_out_raw[:, :, :], a["L0_ffn_w_out"].rearrange("(k p) n -> p k n", k=2))
            load(ld_lin, w_qkv1_raw[:, :, :], a["L1_attn_Wqkv"].rearrange("(k p) n -> p k n", k=2))
            load_column(ld_lin, ln_wb[:, :, 0], a["L1_attn_ln_w"].rearrange("(k p) -> p k", k=2))
            load_column(ld_lin, ln_wb[:, :, 1], a["L1_attn_ln_b"].rearrange("(k p) -> p k", k=2))
            load(ld_lin, b_qkv1[:, :], row(a["L1_attn_bqkv"]))
            load(ld_lin, w_g2[:, :, :], a["L1_attn_Wb2"].rearrange("p (h n) -> p h n", n=GATES))
            load(ld_lin, temp[:, :], a["L1_attn_temperature"].partition_broadcast(ROWS))
            load(ld_lin, w_p1_raw[:, :, :], a["L1_attn_Wproj"].rearrange("(k p) n -> p k n", k=2))
            load(ld_lin, b_p1[:, :], row(a["L1_attn_bproj"]))
            for h in range(HALF // HEAD1):
                load_column(ld_lin, mn_wb[h * HEAD1:(h + 1) * HEAD1, 0:1], a["L1_attn_mn_w"].rearrange("(n o) -> n o", o=1))
                load_column(ld_lin, mn_wb[h * HEAD1:(h + 1) * HEAD1, 1:2], a["L1_attn_mn_b"].rearrange("(n o) -> n o", o=1))
            load(ld_lin, w1_raw[:, :], a["L1_ffn_W1"])
            load(ld_lin, w2_raw[:, :, :], a["L1_ffn_W2"].rearrange("(k p) n -> p k n", k=2))
            load(ld_lin, wo_raw[:, :, :], a["L1_ffn_Wo"].rearrange("(k p) n -> p k n", k=2))
            load_column(ld_lin, b2_col[:, :], a["L1_ffn_b2"].rearrange("(k p) -> p k", k=2))
            load(ld_lin, bo[:, :], row(a["L1_ffn_bo"]))
            load(ld_att, w_o0[:, :, :], a["L0_attn_w_out"].rearrange("(k p) n -> p k n", p=128))
            load(ld_att, g_in[:, :], a["L0_ffn_g_in"].partition_broadcast(ROWS))
            load(ld_att, g_out[:, :], a["L0_ffn_g_out"].partition_broadcast(ROWS))
            load(ld_late, w_g1[:, :, :], a["L1_attn_Wb1"].rearrange("(k p) n -> p k n", k=2))
            load(ld_late, gamma[:, :], a["L1_ffn_gamma"].partition_broadcast(ROWS))
            load(ld_late, beta[:, :], a["L1_ffn_beta"].partition_broadcast(ROWS))
            load(ld_late, w1[HALF:HALF + 1, 0, :], row(a["L1_ffn_b1"]))
            for g in range(2, 4):
                load_strips(g, g % 2)
            sp.wait_ge(setup_row, 1)
            load(ld_late, w_qkv1[HALF:HALF + 1, 0, :], b_qkv1[:, :])
            sp.wait_ge(setup_row, 2)
            load(ld_late, w_p1[HALF:HALF + 1, 0, :], b_p1[:, :])
            with sp.Fori(2, GROUPS // 2) as pair:
                load_strips(2 * pair, 0)
                load_strips(2 * pair + 1, 1)
            load_strips(GROUPS - 1, (GROUPS - 1) % 2)

        @block.gpsimd
        def _(pool):
            pool.memset(ones[:, :], 1.0)
            pool.memset(minus_half[:, :], -0.5)
            for n, value in enumerate((1.0 + EPS_RMS, EPS * EPS_RMS, 1.0, 1.0 + EPS, EPS, EPS * EPS, EPS, EPS_RMS)):
                pool.memset(gain_eps[:, n:n + 1], value)
            gain1, eps1, gain2, eps2 = gain_eps[0:ROWS, 0:1], gain_eps[0:ROWS, 1:2], gain_eps[0:ROWS, 2:4], gain_eps[0:ROWS, 4:6]
            eps_ln, eps_rms = gain_eps[0:ROWS, 6:7], gain_eps[0:ROWS, 7:8]
            pool.memset(eps_head[:, :], HEAD1 * EPS)
            for n, c in enumerate(sine_coefficients()):
                pool.memset(sine_terms[:, n, :], c)
            pool.memset(pad_pool[:, :], 0.0)
            pool.memset(patchT[:, :, :], 0.0)
            pool.memset(scores[:, :, :], FILLER)
            pool.memset(v1[:, :, :], 1.0)
            pool.memset(norms2T[:, :, :], 1.0)
            pool.memset(att1T[:, :, :], 1.0)
            pool.memset(norm3T[:, :, :], 1.0).then_inc(setup_pool, 1)
            pool.wait_ge(setup_pool, 1)
            pool.wait_ge(ld_bias, 16)
            setup = [lambda: pool.wait_ge(ld_att, 48), lambda: None, lambda: late_setup(pool)]

            in_chain = chain_of(pool, RUN["p_ffn"], 2)
            norms_chain = chain_of(pool, RUN["p_lin"], 2)
            gate_chain = chain_of(pool, RUN["p_gate"], 2 * SINE_ORDER + 5)
            last_chain = chain_of(pool, RUN["p_last"], 2)

            def rstd(g, chain, rstd_ready, var, spread, rstd_out, eps):
                chain(g, pool.tensor_tensor(spread, var, eps, ALU.add))
                pool.tensor_tensor(rstd_out, spread, minus_half[0:ROWS, 0:spread.shape[1]], ALU.pow) \
                    .then_inc(rstd_ready, 1)

            def p_strips(g, p):
                pool.wait_ge(strips_in[p], 16 * (g // 2 + 1) if isinstance(g, int) else 8 * (g - p) + 16)
                after(pool, S["patches1"], g)
                pool.tensor_tensor(pad_pool[:, :], pad_pool[:, :], ones[:, 0:1], ALU.mult)
                pool.tensor_copy(patches[:, :, :].rearrange("p x (r c) -> p x r c", r=PATCH),
                                 strips[:, p].rearrange("p r (x c) -> p x r c", x=GRID)).then_inc(S["strips_cut"], 1)

            def p_rstd0(g, p):
                pool.wait_ge(S["moments0"], g + 1)
                rstd(g, chain_of(pool, S["spread0"], 1), S["rstd0"], moments0[:, 1:2], spread0[:, :], rstd0[:, :], eps_ln)

            def p_h0(g, p):
                pool.wait_ge(S["norm0"], g + 1)
                pool.tensor_tensor(h0[:, p], h0[:, p], b_o0[:, :], ALU.add).then_inc(S["h0_biased"], 1)

            def p_rstd1(g, p):
                pool.wait_ge(S["moments1"], g + 1)
                in_chain(g, pool.tensor_tensor(spread1[:, 0:1], moments1[:, 1:2], gain1, ALU.mult))
                rstd(g, in_chain, S["rstd1"], spread1[:, 0:1], spread1[:, 1:2], rstd1[:, :], eps1)

            def p_rms(g, p):
                pool.wait_ge(S["square_sum"], g + 1)
                rstd(g, chain_of(pool, S["mean_square"], 1), S["rms_inv"], square_sum[:, :], mean_square[:, :], rms_inv[:, :], eps_rms)

            def p_scaled(g, p):
                pool.wait_ge(S["product"], g + 1)
                pool.tensor_tensor(scaled[:, :], product[:, :], g_out[:, :], ALU.mult).then_inc(S["scaled"], 1)

            def p_rstd2(g, p):
                pool.wait_ge(S["moments2"], g + 1)
                norms_chain(g, pool.tensor_tensor(spread2[:, 0], moments2[:, 1:2].to_broadcast([ROWS, 2]), gain2, ALU.mult))
                rstd(g, norms_chain, S["rstd2"], spread2[:, 0], spread2[:, 1], rstd2[:, :], eps2)

            def p_feat_k(g, p):
                pool.wait_ge(S["feat_k_all"], g + 1)
                for odd in range(2):
                    keep = consts[0:HALF, C_PARITY + odd:C_PARITY + odd + 1].unsqueeze(2).to_broadcast([HALF, 2, ROWS])
                    last = pool.tensor_tensor(feat_k[:, odd], feat_qk[:, 2:4, :], keep, ALU.mult)
                last.then_inc(S["feat_k"], 1)

            def p_gate(g, p):
                pool.wait_ge(S["tanh_par"], g + 1)
                for n in range(2):
                    pool.tensor_tensor(amp[:, n], tanh_par[:, :, 2 * n], ones[0:ROWS, 0:HEADS], ALU.add)
                gate_chain(g, pool.tensor_tensor(wave[:, :], tanh_par[:, :, 1], tanh_par[:, :, 3], ALU.subtract))
                pool.tensor_tensor(amps[:, :], amp[:, 0], amp[:, 1], ALU.mult)
                gate_chain(g, pool.tensor_tensor(wave_sq[:, :], wave[:, :], wave[:, :], ALU.mult))
                gate_chain(g, pool.tensor_tensor(poly[:, 1], sine_terms[0:ROWS, 0], wave_sq[:, :], ALU.mult))
                for n in range(1, SINE_ORDER + 1):
                    gate_chain(g, pool.tensor_tensor(poly[:, 0], poly[:, 1], sine_terms[0:ROWS, n], ALU.add))
                    if n < SINE_ORDER:
                        gate_chain(g, pool.tensor_tensor(poly[:, 1], poly[:, 0], wave_sq[:, :], ALU.mult))
                gate_chain(g, pool.tensor_tensor(sine[:, :], poly[:, 0], wave[:, :], ALU.mult))
                gate_chain(g, pool.tensor_tensor(sine_sq[:, :], sine[:, :], sine[:, :], ALU.mult))
                gate_chain(g, pool.tensor_tensor(cosine[:, :], ones[0:ROWS, 0:HEADS], sine_sq[:, :], ALU.subtract))
                pool.tensor_tensor(overlap[:, :], cosine[:, :], amps[:, :], ALU.mult).then_inc(S["overlap"], 1)

            def p_centred_sq(g, p):
                pool.wait_ge(S["centred"], g + 1)
                pool.tensor_tensor(centred_sq[:, :, :], centred[:, :, :], centred[:, :, :], ALU.mult) \
                    .then_inc(S["centred_sq"], 1)

            def p_rstd_h(g, p):
                pool.wait_ge(S["sq_sum"], g + 1)
                rstd(g, chain_of(pool, RUN["p_head"], 1), S["rstd_h"], sq_sum[:, :], spread_h[:, :], rstd_h[:, :], eps_head[0:ROWS, :])

            def p_rstd3(g, p):
                pool.wait_ge(S["moments3"], g + 1)
                rstd(g, last_chain, S["rstd3"], moments3[:, 1:2], spread3[:, :], rstd3[:, :], eps_ln)

            def p_h3_beta(g, p):
                pool.wait_ge(S["h3"], g + 1)
                pool.tensor_tensor(h3_beta[:, :], h3[:, p], beta[:, :], ALU.add).then_inc(S["h3_beta"], 1)

            def p_rstd4(g, p):
                pool.wait_ge(S["moments4"], g + 1)
                rstd(g, last_chain, S["rstd4"], moments4[:, 1:2], spread4[:, :], rstd4[:, :], eps_ln)

            iterations(pool, lambda i, parity, active: in_turn(i, parity, active, [
                (0, p_strips), (4, p_feat_k), (4, p_gate), (3, p_scaled), (3, p_rms), (5, p_rstd4),
                (4, p_centred_sq), (4, p_rstd_h), (1, p_h0), (0, p_rstd0), (3, p_rstd2), (2, p_rstd1), (4, p_rstd3),
                (4, p_h3_beta),
            ]), setup)

        @block.vector
        def _(dve):
            done = [0]

            def link(instruction):
                done[0] += 1
                instruction.then_inc(setup_dve, 1)
                dve.wait_ge(setup_dve, done[0])

            dve.wait_ge(ld_const, 16)
            dve.wait_ge(setup_pool, 1)
            dve.tensor_copy(ident_b[:, :], ident)
            link(dve.tensor_copy(score_mask_b[:, :], consts[0:ROWS, C_SCORE:C_SCORE + ROWS]))
            dve.wait_ge(ld_qkv, 32)
            link(dve.tensor_scalar(scale_b[:, :], scale_b[:, :], -1.0, None, ALU.mult))
            for k in range(2):
                wq = w_qkv0[:, k, 0:INNER].rearrange("p (h d) -> p h d", h=HEADS)
                link(dve.tensor_tensor(wq, wq, scale_b[:, :].unsqueeze(2).to_broadcast([HALF, HEADS, HEAD0]), ALU.mult))
            dve.wait_ge(setup_pe, 1)
            link(dve.tensor_copy(start[:, :], M1[0:ROWS, 0:EMBED]))
            dve.memset(pad[:, :], 0.0).then_inc(ready, 1)

            def setup_ffn():
                dve.wait_ge(ld_ffn, 32)
                link(dve.memset(abs_sums[:, :], 0.0))
                flat_in = w_in_raw[:, :, :].rearrange("p k n -> p (k n)")
                flat_out = w_out_raw[:, :, :].rearrange("p k n -> p (k n)")
                dve.tensor_reduce(abs_sums[:, 0:1], flat_in, X, ALU.add, apply_absolute_value=True)
                dve.tensor_reduce(abs_sums[0:HALF, 1:2], flat_out, X, ALU.add, apply_absolute_value=True) \
                    .then_inc(setup_sums, 1)
                dve.wait_ge(setup_pe, 2)
                link(dve.tensor_scalar(w_scale[:, 0:1], M0[:, 0:1], 1.0 / (2 * HIDDEN0 * EMBED), EPS_QUANT, ALU.mult, ALU.max))
                link(dve.tensor_scalar(w_scale[:, 1:2], M0[:, 1:2], 1.0 / (HIDDEN0 * EMBED), EPS_QUANT, ALU.mult, ALU.max))
                link(dve.reciprocal(w_scale_inv[:, :], w_scale[:, :]))
                link(dve.tensor_scalar(w_scale_127[:, :], w_scale[:, :], 1.0 / 127.0, None, ALU.mult))
                for flat, n, q in ((flat_in, 0, w_in_q[:, :, :]), (flat_out, 1, w_out_q[:, :, :])):
                    rows = flat.shape[0]
                    link(dve.tensor_scalar(flat, flat, w_scale_inv[0:rows, n:n + 1], ROUND, ALU.mult, ALU.add))
                    link(dve.tensor_scalar(flat, flat, -ROUND, 1.0, ALU.add, ALU.min))
                    link(dve.tensor_scalar(q.rearrange("p k n -> p (k n)"), flat, -1.0, None, ALU.max))
                link(dve.memset(pad[:, :], 0.0))
                dve.memset(pad[:, :], 0.0).then_inc(setup_ternary, 1)
                dve.wait_ge(ld_att, 48)

            def setup_gains():
                dve.wait_ge(ld_lin, 16 * 25)
                for k in range(2):
                    link(dve.tensor_scalar(w_qkv1[0:HALF, k, :], w_qkv1_raw[:, k, :], ln_wb[:, k, 0:1], None, ALU.mult))
                    link(dve.tensor_scalar(w_p1[0:HALF, k, :], w_p1_raw[:, k, :], mn_wb[:, 0:1], HEAD1 ** 0.5, ALU.mult, ALU.mult))
                link(dve.tensor_scalar(w_g2[:, :, :], w_g2[:, :, :], 0.5, None, ALU.mult))
                for n in (0, 2):
                    link(dve.tensor_scalar(w_g2[:, :, n], w_g2[:, :, n], 0.5, None, ALU.mult))
                link(dve.tensor_scalar(temp[:, :], temp[:, :], 0.1, 2.0, ALU.max, ALU.min))
                link(dve.tensor_scalar(temp[:, :], temp[:, :], 0.5, None, ALU.mult))

            def setup_biases():
                dve.wait_ge(setup_pe, 3)
                dve.tensor_tensor(b_qkv1[:, 0:384], L0[0:1, 0:384], b_qkv1[:, 0:384], ALU.add)
                dve.tensor_tensor(b_qkv1[:, 384:576], L1[0:1, 0:192], b_qkv1[:, 384:576], ALU.add).then_inc(setup_row, 1)
                dve.tensor_tensor(b_p1[:, :], L1[0:1, 192:384], b_p1[:, :], ALU.add).then_inc(setup_row, 1)
                dve.wait_ge(setup_pe, 4)
                dve.tensor_copy(w2o[:, :], M1[:, 0:EMBED])
                dve.tensor_tensor(b2o_row[:, :], M1[0:1, EMBED:2 * EMBED], bo[:, :], ALU.add).then_inc(setup_row, 1)
                dve.wait_ge(setup_pe, 5)
                link(dve.tensor_copy(b2o[:, :], M0[0:ROWS, 0:EMBED]))
                dve.wait_ge(setup_row, 3)
                link(dve.memset(pad[:, :], 0.0))
                dve.memset(pad[:, :], 0.0).then_inc(ready, 1)
                late_setup(dve)

            setup = [setup_ffn, setup_gains, setup_biases]

            att_chain = chain_of(dve, RUN["v_att"], 7)
            in_chain = chain_of(dve, RUN["v_in"], 6)
            out_chain = chain_of(dve, RUN["v_out"], 6)
            lin_chain = chain_of(dve, RUN["v_lin"], 4)
            last_chain = chain_of(dve, RUN["v_last"], 2)

            def stats(g, chain, stats_tile, moments, moments_ready, src):
                chain(g, dve.bn_stats(stats_tile[:, :], src))
                dve.memset(pad[0:ROWS, :], 0.0)
                dve.bn_aggr(moments[:, :], stats_tile[:, :]).then_inc(moments_ready, 1)

            def v_h0(g, p):
                dve.wait_ge(S["embedded"], g + 1)
                dve.tensor_tensor(h0[:, p], E0[0:ROWS, 0:EMBED], start[:, :], ALU.add).then_inc(S["h0_copied"], 1)

            def v_stats0(g, p):
                dve.wait_ge(S["h0_copied"], g + 1)
                stats(g, chain_of(dve, S["stats0"], 1), stats0, moments0, S["moments0"], h0[:, p])

            def v_norm0(g, p):
                dve.wait_ge(S["rstd0"], g + 1)
                after(dve, S["norm0_turned"], g)
                dve.tensor_scalar(norm0[:, :], h0[:, p], moments0[:, 0:1], rstd0[:, 0:1],
                                  ALU.subtract, ALU.mult).then_inc(S["norm0"], 1)

            def v_pack(f, src):
                def step(g, p):
                    dve.wait_ge(dots[f // 2], g + 1)
                    place = QTILES * (f % 2) + 3 * (f // 2)
                    dve.tensor_reduce(scores[:, place:place + 3, TOKENS - 1::-1],
                                      src[0:ROWS, 0:3 * ROWS].rearrange("p (h b j) -> p h j b", h=3, b=PER),
                                      X, ALU.max).then_inc(packed[f], 1)
                return step

            def v_top(g, p):
                for f in range(4):
                    dve.wait_ge(packed[f], g + 1)
                dve.tensor_reduce(score_sum[:, :], scores[:, :, 0:TOKENS].rearrange("p h j -> p j h"), X, ALU.add)
                for h in range(HEADS):
                    last = dve.max(top[:, h, :], scores[:, h, 0:TOKENS])
                att_chain(g, last)
                att_chain(g, dve.memset(top[:, :, DROP + 1:8], FILLER))

            def v_drop(g, p):
                dve.memset(pad_drop[0:ROWS, :], 0.0)
                for h in range(HEADS):
                    last = dve.match_replace(kept[:, h, :], top[:, h, :], scores[:, h, :], BIG)
                att_chain(g, last)

            def v_mix(g, p):
                att_chain(g, dve.scalar_tensor_tensor(
                    mixed[:, :, :], score_sum[:, :].unsqueeze(1).to_broadcast([ROWS, HEADS, TOKENS]),
                    1.0 / HEADS, kept[:, :, 0:TOKENS], ALU.mult, ALU.add))
                att_chain(g, dve.tensor_reduce(least[:, :], mixed[:, :, :], X, ALU.min))
                dve.tensor_tensor(shifted[:, :, :], mixed[:, :, :],
                                  least[:, :].unsqueeze(2).to_broadcast([ROWS, HEADS, TOKENS]),
                                  ALU.subtract).then_inc(S["shifted"], 1)

            def v_probs(g, p):
                dve.wait_ge(S["expd"], g + 1)
                att_chain(g, dve.tensor_reduce(exp_sum[:, :], expd[:, :, :], X, ALU.add))
                att_chain(g, dve.reciprocal(exp_inv[:, :], exp_sum[:, :]))
                dve.tensor_tensor(probs[:, :, :], expd[:, :, ::-1],
                                  exp_inv[:, :].unsqueeze(2).to_broadcast([ROWS, HEADS, TOKENS]),
                                  ALU.mult).then_inc(S["probs"], 1)

            def masked(turned, mask, dst, ready_sem, src):
                def step(g, p):
                    dve.wait_ge(turned, g + 1)
                    dve.tensor_tensor(dst, parts(src, 4)[0:ROWS], mask.unsqueeze(1).to_broadcast([ROWS, 4, ROWS]),
                                      ALU.mult).then_inc(ready_sem, 1)
                return step

            def v_wide(f):
                def step(g, p):
                    dve.wait_ge(S["probs"], g + 1)
                    if f == 0:
                        after(dve, S["turned2"], g)
                    dve.tensor_tensor(
                        wide[:, 4 * f:4 * f + 4], probs[:, 4 * f:4 * f + 4, :].unsqueeze(2).to_broadcast([ROWS, 4, PER, TOKENS]),
                        block_mask.rearrange("p (b j) -> p b j", b=PER).unsqueeze(1).to_broadcast([ROWS, 4, PER, TOKENS]),
                        ALU.mult).then_inc((S["widened0"], S["widened1"], S["widened2"])[f], 1)
                return step

            def v_h1(g, p):
                dve.wait_ge(S["h0_biased"], g + 1)
                dve.wait_ge(S["proj0"], g + 1)
                dve.tensor_tensor(h1[:, p], A1[0:ROWS, 0:EMBED], h0[:, p], ALU.add).then_inc(S["h1"], 1)

            def v_u_in(g, p):
                dve.wait_ge(S["h1"], g + 1)
                stats(g, in_chain, stats1, moments1, S["moments1"], h1[:, p])
                dve.wait_ge(S["moments1"], g + 1)
                in_chain(g, dve.scalar_tensor_tensor(u_in[:, :], h1[:, p], moments1[:, 0:1], g_in[:, :],
                                                      ALU.subtract, ALU.mult))
                in_chain(g, dve.tensor_reduce(umax_in[:, :], u_in[:, :], X, ALU.max, apply_absolute_value=True))

            def v_big_in(g, p):
                dve.wait_ge(S["rstd1"], g + 1)
                in_chain(g, dve.tensor_scalar(amax_in[:, :], umax_in[:, :], rstd1[:, 0:1], EPS_QUANT, ALU.mult, ALU.max))
                dve.tensor_scalar(unit_in[:, 1:2], amax_in[:, :], w_scale_127[0:ROWS, 0:1], None, ALU.mult)
                dve.tensor_scalar(unit_in[:, 0:1], amax_in[:, :], w_scale_127[0:ROWS, 0:1], 0.5, ALU.mult, ALU.mult) \
                    .then_inc(S["unit_in"], 1)
                in_chain(g, dve.reciprocal(ainv_in[:, :], amax_in[:, :]))
                in_chain(g, dve.tensor_scalar(quant_in[:, :], ainv_in[:, :], rstd1[:, 0:1], 127.0, ALU.mult, ALU.mult))
                dve.tensor_scalar(big_in[:, :], u_in[:, :], quant_in[:, 0:1], ROUND, ALU.mult, ALU.add) \
                    .then_inc(S["big_in"], 1)
                dve.tensor_scalar(half_c2[:, 0:1], unit_in[:, 0:1], unit_in[:, 1:2], None, ALU.mult)
                dve.tensor_scalar(half_c2[:, 1:2], unit_in[:, 0:1], unit_in[:, 1:2], HIDDEN0 ** -0.5, ALU.mult, ALU.mult) \
                    .then_inc(S["half_c2"], 1)

            def v_gated(g, p):
                dve.wait_ge(S["tanh_gate"], g + 1)
                out_chain(g, dve.scalar_tensor_tensor(gated[:, :], tanh_gate[:, :], 1.0, M1[0:ROWS, :], ALU.add, ALU.mult))
                dve.wait_ge(S["up_done"], g + 1)
                dve.tensor_tensor(product[:, :], M0[0:ROWS, :], gated[:, :], ALU.mult).then_inc(S["product"], 1)

            def v_big_out(g, p):
                dve.wait_ge(S["scaled"], g + 1)
                out_chain(g, dve.tensor_reduce(umax_out[:, :], scaled[:, :], X, ALU.max, apply_absolute_value=True))
                dve.wait_ge(S["rms_inv"], g + 1)
                out_chain(g, dve.tensor_scalar(row_gain[:, :], rms_inv[:, :], half_c2[:, 0:1], None, ALU.mult))
                out_chain(g, dve.tensor_scalar(amax_out[:, :], umax_out[:, :], row_gain[:, 0:1], EPS_QUANT, ALU.mult, ALU.max))
                dve.tensor_scalar(unit_out[:, :], amax_out[:, :], w_scale_127[0:ROWS, 1:2], None, ALU.mult)
                out_chain(g, dve.reciprocal(ainv_out[:, :], amax_out[:, :]))
                out_chain(g, dve.tensor_scalar(quant_out[:, :], ainv_out[:, :], row_gain[:, 0:1], 127.0, ALU.mult, ALU.mult))
                dve.tensor_scalar(big_out[:, :], scaled[:, :], quant_out[:, 0:1], ROUND, ALU.mult, ALU.add) \
                    .then_inc(S["big_out"], 1)

            def v_h2(g, p):
                dve.wait_ge(S["down_done"], g + 1)
                dve.scalar_tensor_tensor(h2[:, p], M0[0:ROWS, 0:EMBED], unit_out[:, 0:1], h1[:, p],
                                         ALU.mult, ALU.add).then_inc(S["h2"], 1)

            def v_stats2(g, p):
                dve.wait_ge(S["h2"], g + 1)
                stats(g, chain_of(dve, S["stats2"], 1), stats2, moments2, S["moments2"], h2[:, p])

            def v_norms2(g, p):
                dve.wait_ge(S["rstd2"], g + 1)
                for n in range(2):
                    last = dve.tensor_scalar(norms2[:, n], h2[:, p], moments2[:, 0:1], rstd2[:, n:n + 1],
                                             ALU.subtract, ALU.mult)
                last.then_inc(S["norms2"], 1)

            def v_hidT(g, p):
                dve.wait_ge(S["tanh_hid"], g + 1)
                dve.scalar_tensor_tensor(hidT[:, :], tanh_hid[:, :], 1.0, L0[:, 0:ROWS], ALU.add, ALU.mult) \
                    .then_inc(S["hidT"], 1)

            def v_feat(g, p):
                dve.wait_ge(S["relu_qk"], g + 1)
                for n, ready_sem in ((2, S["feat_k_all"]), (0, S["feat_q"])):
                    dve.scalar_tensor_tensor(feat_qk[:, n:n + 2, :], exp_qk[:, n:n + 2, :], 1.0, relu_qk[:, n:n + 2, :],
                                             ALU.min, ALU.add).then_inc(ready_sem, 1)

            def v_v1(g, p):
                dve.wait_ge(S["tanh_int"], g + 1)
                dve.scalar_tensor_tensor(v1[:, :, 0:HEAD1], tanh_int[:, :].unsqueeze(2).to_broadcast([ROWS, HEADS, HEAD1]), 3.0,
                                         v_raw[:, :, :], ALU.add, ALU.mult).then_inc(S["v1"], 1)

            def v_ratio(g, p):
                num = L0[0:ROWS, 0:HEADS * SLOT].rearrange("p (h d) -> p h d", h=HEADS)
                dve.wait_ge(S["num"], g + 1)
                lin_chain(g, dve.tensor_scalar(den[:, :], num[:, :, HEAD1], 2.0, 2 * EPS_DEN, ALU.mult, ALU.add))
                lin_chain(g, dve.reciprocal(den_inv[:, :], den[:, :]))
                lin_chain(g, dve.tensor_tensor(ratio[:, :, :], num[:, :, 0:HEAD1],
                                               den_inv[:, :].unsqueeze(2).to_broadcast([ROWS, HEADS, HEAD1]), ALU.mult))
                lin_chain(g, dve.tensor_reduce(ratio_sum[:, :], ratio[:, :, :], X, ALU.add))
                dve.scalar_tensor_tensor(centred[:, :, :], ratio_sum[:, :].unsqueeze(2).to_broadcast([ROWS, HEADS, HEAD1]),
                                         -1.0 / HEAD1, ratio[:, :, :], ALU.mult, ALU.add).then_inc(S["centred"], 1)

            def v_sq_sum(g, p):
                dve.wait_ge(S["centred_sq"], g + 1)
                dve.tensor_reduce(sq_sum[:, :], centred_sq[:, :, :], X, ALU.add).then_inc(S["sq_sum"], 1)

            def v_att1(g, p):
                dve.wait_ge(S["rstd_h"], g + 1)
                dve.tensor_tensor(att1[:, :, :], centred[:, :, :],
                                  rstd_h[:, :].unsqueeze(2).to_broadcast([ROWS, HEADS, HEAD1]), ALU.mult) \
                    .then_inc(S["att1"], 1)

            def v_h3(g, p):
                dve.wait_ge(S["proj1"], g + 1)
                dve.tensor_tensor(h3[:, p], L0[0:ROWS, 256:256 + EMBED], h2[:, p], ALU.add).then_inc(S["h3"], 1)

            def v_stats3(g, p):
                dve.wait_ge(S["h3"], g + 1)
                stats(g, last_chain, stats3, moments3, S["moments3"], h3[:, p])

            def v_norm3(g, p):
                dve.wait_ge(S["rstd3"], g + 1)
                dve.tensor_scalar(norm3[:, :], h3[:, p], moments3[:, 0:1], rstd3[:, 0:1],
                                  ALU.subtract, ALU.mult).then_inc(S["norm3"], 1)

            def v_stats4(g, p):
                dve.wait_ge(S["out4"], g + 1)
                dve.tensor_tensor(out4[:, :], M1[0:ROWS, 0:EMBED], b2o[:, :], ALU.add).then_inc(S["out4_copied"], 1)
                dve.wait_ge(S["out4_copied"], g + 1)
                stats(g, last_chain, stats4, moments4, S["moments4"], out4[:, :])
                dve.wait_ge(S["moments4"], g + 1)
                dve.scalar_tensor_tensor(scaled4[:, :], out4[:, :], moments4[:, 0:1], gamma[:, :],
                                         ALU.subtract, ALU.mult).then_inc(S["scaled4"], 1)

            def v_result(g, p):
                dve.wait_ge(S["rstd4"], g + 1)
                dve.wait_ge(S["scaled4"], g + 1)
                dve.wait_ge(S["h3_beta"], g + 1)
                after(dve, stored[p], 16 * (g // 2) if isinstance(g, int) else 8 * (g - p))
                dve.scalar_tensor_tensor(result[:, p], scaled4[:, :], rstd4[:, 0:1], h3_beta[:, :],
                                         ALU.mult, ALU.add).then_inc(S["result"], 1)

            dots = [S["dots01"], S["dots23"]]
            packed = [S["packed0"], S["packed1"], S["packed2"], S["packed3"]]
            v_causal = [masked(t, causal_mask, weightsT[:, 4 * f:4 * f + 4, :], m, src) for f, (t, m, src) in enumerate(
                ((S["a_done01"], S["a_masked0"], L1), (S["a_done01"], S["a_masked1"], L0), (S["a_done2"], S["a_masked2"], L1)))]

            iterations(dve, lambda i, parity, active: in_turn(i, parity, active, [
                (2, v_mix), (3, v_big_in), (4, v_hidT), (4, v_feat), (2, v_probs), (2, v_wide(0)), (2, v_wide(2)),
                (5, v_stats4), (2, v_wide(1)), (4, v_causal[1]), (4, v_causal[0]), (3, v_gated), (4, v_causal[2]),
                (4, v_v1), (3, v_big_out), (4, v_ratio), (5, v_result), (2, v_h1), (4, v_sq_sum), (2, v_u_in),
                (1, v_pack(0, A0)), (1, v_pack(1, A1)), (4, v_att1), (0, v_h0), (0, v_stats0), (3, v_h2),
                (3, v_stats2), (0, v_norm0), (1, v_pack(3, A1)), (1, v_pack(2, A0)), (3, v_norms2), (4, v_h3),
                (1, v_top), (4, v_stats3), (1, v_drop), (4, v_norm3),
            ]), setup)

        @block.scalar
        def _(act):
            copied = [0]

            def evac(dst, src, turned):
                act.wait_ge(setup_turned, turned)
                act.copy(dst, src).then_inc(setup_act, 1)
                copied[0] += 1

            for k in range(0, CHUNKS, 2):
                evac(w_tok[:, k:k + 2, :], (E0 if k % 4 == 0 else E1)[:, 0:2 * EMBED].rearrange("p (k n) -> p k n", k=2), k // 2 + 1)
            act.wait_ge(setup_pool, 1)

            def setup_turned_weights():
                evac(w1[0:HALF, :, :], L0[0:HALF, 0:2 * HIDDEN1].rearrange("p (k n) -> p k n", k=2), 4)
                evac(wo[:, :, :], L1[0:HALF, 0:2 * EMBED].rearrange("p (k n) -> p k n", k=2), 5)
                for n in range(4):
                    src = (M0, M1)[n % 2][:, :].bitcast(BF16)[0:HALF, 0:512].rearrange("p (k n) -> p k n", k=2)
                    evac(w_in[:, :, 256 * n:256 * n + 256], src, 6 + n)
                for n in range(2):
                    src = (M0, M1)[n % 2][:, :].bitcast(BF16)[:, 0:2 * EMBED].rearrange("p (k n) -> p k n", k=2)
                    evac(w_out[:, 2 * n:2 * n + 2, :], src, 10 + n)

            def setup_ready():
                act.wait_ge(setup_act, copied[0])
                act.copy(pad_act[:, :], ones[:, 0:1]).then_inc(ready, 1)
                late_setup(act)

            setup = [lambda: None, setup_turned_weights, setup_ready]

            def copy_step(waits, dst, src, done_sem):
                def step(g, p):
                    for w in waits:
                        act.wait_ge(w, g + 1)
                    act.copy(dst, src).then_inc(done_sem, 1)
                return step

            def a_patchT(n, bank_tile, turned, done_sem):
                def step(g, p):
                    act.wait_ge(turned, g + 1)
                    if n == 0:
                        after(act, S["embedded"], g)
                    act.copy(patchT[:, n::2, :].rearrange("p c (b t) -> p c b t", t=TOKENS)[:, :, :, 1:TOKENS],
                             bank_tile[:, 0:STRIPS * GRID].rearrange("p (b c t) -> p c b t", b=PER, c=CHANNELS)) \
                        .then_inc(done_sem, 1)
                return step

            def a_norm0T(g, p):
                act.wait_ge(S["norm0_turned"], g + 1)
                act.copy(norm0T[:, :, :], parts(E1, 2)[0:HALF]).then_inc(S["norm0T"], 1)

            def a_v(n):
                def step(g, p):
                    act.wait_ge((S["v_half0"], S["v_half1"])[n], g + 1)
                    if n == 0:
                        after(act, S["att_done1"], g - 1)
                    act.copy(v0[:, p, n * 384:(n + 1) * 384], (E0, E1)[n][0:ROWS, 0:384]) \
                        .then_inc((S["v_copied0"], S["v_copied1"])[n], 1)
                return step

            def a_qk(n):
                def step(g, p):
                    act.wait_ge((S["qk_done0"], S["qk_done1"], S["qk_done2"])[n], g + 1)
                    if n == 0:
                        after(act, S["dots23"], g - 1)
                    act.copy(qkT[:, p, 4 * n:4 * n + 4, :], parts((E0, E1, E0)[n], 4)) \
                        .then_inc((S["qk_copied0"], S["qk_copied1"], S["qk_copied2"])[n], 1)
                return step

            def a_exp(g, p):
                act.wait_ge(S["shifted"], g + 1)
                act.activation(expd[:, :, :], shifted[:, :, :], ACT.Exp, scale=-1.0).then_inc(S["expd"], 1)

            a_probsT = [copy_step([(S["turned0"], S["turned1"], S["turned2"])[f]], probsT[:, 4 * f:4 * f + 4, :],
                                  parts((A0, A1, A0)[f], 4)[0:ROWS], (S["probsT0"], S["probsT1"], S["probsT2"])[f]) for f in range(3)]
            a_att = [copy_step([(S["att_done0"], S["att_done1"])[n]], att0T[:, 3 * n:3 * n + 3, :], parts((A1, A0)[n], 3),
                               (S["att_copied0"], S["att_copied1"])[n]) for n in range(2)]

            def a_int_in(g, p):
                act.wait_ge(S["big_in"], g + 1)
                act.activation(int_in[:, :], big_in[:, :], ACT.Copy, bias=-ROUND).then_inc(S["int_in"], 1)

            a_in_T = copy_step([S["in_turned"]], int_inT[:, :, :],
                               M0[:, :].bitcast(BF16)[0:HALF, 0:256].rearrange("p (k n) -> p k n", k=2)[:, :, 0:ROWS],
                               S["in_copied"])

            def a_tanh_gate(g, p):
                act.wait_ge(S["gate_done"], g + 1)
                act.wait_ge(S["unit_in"], g + 1)
                act.activation(tanh_gate[:, :], M1[0:ROWS, :], ACT.Tanh, scale=unit_in[:, 0:1]).then_inc(S["tanh_gate"], 1)

            def a_square(g, p):
                act.wait_ge(S["product"], g + 1)
                act.wait_ge(S["half_c2"], g + 1)
                act.activation(squares[:, :], product[:, :], ACT.Square, scale=half_c2[:, 1:2],
                               accum_out=square_sum[:, :]).then_inc(S["square_sum"], 1)

            def a_int_out(g, p):
                act.wait_ge(S["big_out"], g + 1)
                act.activation(int_out[:, :], big_out[:, :], ACT.Copy, bias=-ROUND).then_inc(S["int_out"], 1)

            a_out_T = copy_step([S["out_turned"]], int_outT[:, :, :],
                                M1[:, :].bitcast(BF16)[:, 0:512].rearrange("p (k n) -> p k n", k=4)[:, :, 0:ROWS],
                                S["out_copied"])

            a_norms_T = copy_step([S["norms_turned"]], norms2T[0:HALF, :, :], parts(L0, 4)[0:HALF], S["norms_copied"])

            def a_qk1(g, p):
                act.wait_ge(S["qk1"], g + 1)
                act.activation(exp_qk[:, :, :], parts(L1, 4)[0:HALF], ACT.Exp)
                act.activation(relu_qk[:, :, :], parts(L1, 4)[0:HALF], ACT.Relu).then_inc(S["relu_qk"], 1)

            def a_tanh_hid(g, p):
                act.wait_ge(S["hid"], g + 1)
                act.activation(tanh_hid[:, :], L0[:, 0:ROWS], ACT.Tanh, scale=0.5)
                act.copy(v_raw[:, :, :], L0[0:ROWS, 128:128 + EMBED].rearrange("p (h d) -> p h d", h=HEADS)) \
                    .then_inc(S["tanh_hid"], 1)

            def a_tanh_par(g, p):
                act.wait_ge(S["params"], g + 1)
                act.activation(tanh_par[:, :, :], L0[0:ROWS, 384:384 + HEADS * GATES].rearrange("p (h n) -> p h n", n=GATES),
                               ACT.Tanh).then_inc(S["tanh_par"], 1)

            def a_interference(g, p):
                act.wait_ge(S["overlap"], g + 1)
                act.activation(tanh_over[:, :], overlap[:, :], ACT.Tanh, scale=0.25).then_inc(S["tanh_over"], 1)
                act.wait_ge(S["tanh_over"], g + 1)
                act.activation(tanh_int[:, :], tanh_over[:, :], ACT.Tanh, scale=temp[:, 0:1]).then_inc(S["tanh_int"], 1)

            a_num_T = copy_step([S["num_done"]], numT[:, :, :], parts(L0, NUM_TILES), S["num_copied"])
            a_att1_T = copy_step([S["att1_turned"]], att1T[0:HALF, :, :], parts(L1, 2)[0:HALF], S["att1_copied"])

            a_norm3_T = copy_step([S["norm3_turned"]], norm3T[0:HALF, :, :], parts(M1, 2)[0:HALF], S["norm3_copied"])

            def a_hid1(g, p):
                act.wait_ge(S["hid1"], g + 1)
                act.activation(hid1T[:, :], M0[:, 0:ROWS], ACT.Relu).then_inc(S["hid1_copied"], 1)

            def a_store(g, p):
                act.wait_ge(S["result"], g + 1)
                if isinstance(g, int) and g == GROUPS - 1:
                    first = (GROUPS - 1) * PER
                    n = (IMAGES - first) * TOKENS
                    act.dma_start(out[first * TOKENS:IMAGES * TOKENS, :], result[ROWS - n:ROWS, p]).then_inc(stored[p], 16)
                else:
                    act.dma_start(out[bass.ds(g * ROWS, ROWS), :], result[:, p]).then_inc(stored[p], 16)

            iterations(act, lambda i, parity, active: in_turn(i, parity, active, [
                (1, a_v(0)), (1, a_v(1)), (2, a_exp), (4, a_qk1), (5, a_norm3_T), (3, a_int_in), (5, a_hid1),
                (4, a_tanh_par), (1, a_qk(0)), (3, a_in_T), (2, a_probsT[0]), (3, a_tanh_gate), (1, a_qk(1)),
                (2, a_probsT[1]), (2, a_probsT[2]), (4, a_interference), (3, a_square), (1, a_qk(2)), (4, a_num_T),
                (2, a_att[0]), (2, a_att[1]), (3, a_int_out), (3, a_out_T), (5, a_store),
                (0, a_patchT(1, E1, S["patches1"], S["patchT1"])), (0, a_patchT(0, E0, S["patches0"], S["patchT0"])),
                (4, a_att1_T), (0, a_norm0T), (3, a_norms_T), (3, a_tanh_hid),
            ]), setup)
            act.wait_ge(stored[0], 16 * ((GROUPS + 1) // 2))
            act.wait_ge(stored[1], 16 * (GROUPS // 2))

        @block.tensor
        def _(pe):
            def turn(dst, src, identity):
                return pe.transpose(dst, src, identity)

            pe.wait_ge(ld_const, 16)
            pe.wait_ge(ld_tok, 48)
            for k in range(0, CHUNKS, 2):
                if k == 4:
                    pe.wait_ge(setup_act, 1)
                for j in range(2):
                    for e in range(2):
                        last = turn((E0 if k % 4 == 0 else E1)[:, j * EMBED + e * HALF:j * EMBED + (e + 1) * HALF],
                                    w_tok_raw[:, e, (k + j) * 128:(k + j + 1) * 128], ident[0:HALF, 0:HALF])
                last.then_inc(setup_turned, 1)
            pe.matmul(M1[0:ROWS, 0:EMBED], token_kind, start_rows[:, :], start=True, stop=True).then_inc(setup_pe, 1)
            pe.wait_ge(setup_act, 3)

            def setup_sums_of_weights():
                pe.wait_ge(setup_pool, 1)
                pe.wait_ge(setup_sums, 1)
                pe.matmul(M0[:, 0:2], ones[:, :], abs_sums[:, :], start=True, stop=True).then_inc(setup_pe, 1)
                pe.wait_ge(ready, READY_FIRST)
                pe.wait_ge(ld_att, 48)

            def setup_turns():
                pe.wait_ge(ld_lin, 16 * 25)
                for k in range(2):
                    last = turn(L0[0:HALF, k * HIDDEN1:(k + 1) * HIDDEN1], w1_raw[:, k * HALF:(k + 1) * HALF], ident)
                last.then_inc(setup_turned, 1)
                for k in range(2):
                    for e in range(2):
                        last = turn(L1[0:HALF, k * EMBED + e * HALF:k * EMBED + (e + 1) * HALF],
                                    wo_raw[:, e, k * HALF:(k + 1) * HALF], ident[0:HALF, 0:HALF])
                last.then_inc(setup_turned, 1)
                pe.wait_ge(setup_ternary, 1)
                for n in range(4):
                    if n >= 2:
                        pe.wait_ge(setup_act, 3 + 2 + n - 1)
                    for k in range(2):
                        for j in range(2):
                            last = turn((M0, M1)[n % 2][:, :].bitcast(BF16)[0:HALF, k * 256 + j * 128:k * 256 + (j + 1) * 128],
                                        w_in_q[:, 2 * n + j, k * HALF:(k + 1) * HALF], ident_b[:, :])
                    last.then_inc(setup_turned, 1)
                for n in range(2):
                    pe.wait_ge(setup_act, 3 + 2 + 3 + n)
                    for k in range(2):
                        for e in range(2):
                            last = turn((M0, M1)[n % 2][:, :].bitcast(BF16)[:, k * EMBED + e * HALF:k * EMBED + (e + 1) * HALF],
                                        w_out_q[:, e, (2 * n + k) * 128:(2 * n + k + 1) * 128], ident_b[0:HALF, 0:HALF])
                    last.then_inc(setup_turned, 1)

            def setup_biases():
                pe.wait_ge(setup_act, 3 + 2)
                for bank_tile, c0, c1 in ((L0, 0, 384), (L1, 384, 576)):
                    for k in range(2):
                        pe.matmul(bank_tile[0:1, 0:c1 - c0], ln_wb[:, k, 1:2], w_qkv1_raw[:, k, c0:c1], start=k == 0, stop=k == 1)
                for k in range(2):
                    last = pe.matmul(L1[0:1, 192:384], mn_wb[:, 1:2], w_p1_raw[:, k, :], start=k == 0, stop=k == 1)
                last.then_inc(setup_pe, 1)
                pe.wait_ge(setup_act, 3 + 2 + 4 + 2)
                for k in range(2):
                    pe.matmul(M1[:, 0:EMBED], w2_raw[:, k, :], wo[:, k, :], start=k == 0, stop=k == 1)
                for k in range(2):
                    last = pe.matmul(M1[0:1, EMBED:2 * EMBED], b2_col[:, k:k + 1], wo[:, k, :], start=k == 0, stop=k == 1)
                last.then_inc(setup_pe, 1)
                pe.wait_ge(setup_row, 3)
                pe.matmul(M0[0:ROWS, 0:EMBED], ones[0:1, 0:ROWS], b2o_row[:, :], start=True, stop=True) \
                    .then_inc(setup_pe, 1)
                late_setup(pe)

            setup = [setup_sums_of_weights, setup_turns, setup_biases]

            def t_patches(n, bank_tile, freed, done_sem):
                def step(g, p):
                    pe.wait_ge(S["strips_cut"], g + 1)
                    after(pe, freed, g)
                    dst = bank_tile[:, 0:STRIPS * GRID].rearrange("p (s x) -> p s x", x=GRID)
                    for x in range(GRID):
                        last = turn(dst[:, :, x], patches[:, x, 128 * n:128 * (n + 1)], ident[0:STRIPS, 0:STRIPS])
                    last.then_inc(done_sem, 1)
                return step

            def t_embed(g, p):
                pe.wait_ge(S["patchT0"], g + 1)
                pe.wait_ge(S["patchT1"], g + 1)
                for k in range(CHUNKS):
                    last = pe.matmul(E0[0:ROWS, 0:EMBED], patchT[:, k, :], w_tok[:, k, :], start=k == 0, stop=k == CHUNKS - 1)
                last.then_inc(S["embedded"], 1)

            def t_norm0(g, p):
                pe.wait_ge(S["norm0"], g + 1)
                for k in range(2):
                    last = turn(parts(E1, 2)[0:HALF, k], norm0[:, k * HALF:(k + 1) * HALF], ident[0:ROWS, 0:ROWS])
                last.then_inc(S["norm0_turned"], 1)

            def t_v(n):
                def step(g, p):
                    pe.wait_ge(S["norm0T"], g + 1)
                    if n == 0:
                        pe.wait_ge(S["h0_copied"], g + 1)
                    for k in range(2):
                        last = pe.matmul((E0, E1)[n][0:ROWS, 0:384], norm0T[:, k, :],
                                         w_qkv0[:, k, 2 * INNER + n * 384:2 * INNER + (n + 1) * 384], start=k == 0, stop=k == 1)
                    last.then_inc((S["v_half0"], S["v_half1"])[n], 1)
                return step

            def t_qk(n):
                def step(g, p):
                    pe.wait_ge((S["v_copied0"], S["v_copied1"], S["qk_copied0"])[n], g + 1)
                    for j in range(4):
                        for k in range(2):
                            tile = 4 * n + j
                            last = pe.matmul(parts((E0, E1, E0)[n], 4)[:, j], w_qkv0[:, k, tile * 128:(tile + 1) * 128],
                                             norm0T[:, k, :], start=k == 0, stop=k == 1)
                    last.then_inc((S["qk_done0"], S["qk_done1"], S["qk_done2"])[n], 1)
                return step

            def t_dots(n):
                def step(g, p):
                    if n == 0:
                        pe.wait_ge(S["qk_copied2"], g + 1)
                        after(pe, S["att_copied1"], g)
                        after(pe, S["h1"], g)
                    else:
                        pe.wait_ge(S["packed0"], g + 1)
                        pe.wait_ge(S["packed1"], g + 1)
                    dst = [parts(A0, 3)[0:ROWS], parts(A1, 3)[0:ROWS]]
                    for odd in range(2):
                        pe.matmul(dst[odd], ident_b[0:ROWS, 0:ROWS],
                                  score_mask_b[:, :].unsqueeze(1).to_broadcast([ROWS, 3, ROWS]),
                                  start=True, stop=False, skip_group_check=True)
                    for j in range(3):
                        for odd in range(2):
                            r, tile = HEAD0 * odd, 3 * n + j
                            last = pe.matmul(dst[odd][:, j], qkT[r:r + HEAD0, p, tile, :],
                                             qkT[r:r + HEAD0, p, QTILES + tile, :],
                                             start=False, stop=j == 2, skip_group_check=True)
                    last.then_inc((S["dots01"], S["dots23"])[n], 1)
                return step

            def t_probs(f):
                def step(g, p):
                    pe.wait_ge((S["widened0"], S["widened1"], S["widened2"])[f], g + 1)
                    if f == 2:
                        pe.wait_ge(S["probsT0"], g + 1)
                    for j in range(4):
                        last = turn(parts((A0, A1, A0)[f], 4)[0:ROWS, j], wide[:, 4 * f + j].rearrange("p b j -> p (b j)"),
                                    ident[0:ROWS, 0:ROWS])
                    last.then_inc((S["turned0"], S["turned1"], S["turned2"])[f], 1)
                return step

            def t_att0(n):
                def step(g, p):
                    for f in range(3):
                        pe.wait_ge((S["probsT0"], S["probsT1"], S["probsT2"])[f], g + 1)
                    if n == 0:
                        pe.wait_ge(S["v_copied1"], g + 1)
                    dst = parts((A1, A0)[n], 3)
                    for j in range(3):
                        for odd in range(2):
                            tile = 3 * n + j
                            head = 2 * tile + odd
                            last = pe.matmul(dst[64 * odd:64 * odd + 64, j], v0[:, p, head * HEAD0:(head + 1) * HEAD0],
                                             probsT[:, QTILES * odd + tile, :], start=True, stop=True)
                    last.then_inc((S["att_done0"], S["att_done1"])[n], 1)
                return step

            def t_proj0(g, p):
                pe.wait_ge(S["att_copied0"], g + 1)
                for t in range(QTILES):
                    if t == 3:
                        pe.wait_ge(S["att_copied1"], g + 1)
                    last = pe.matmul(A1[0:ROWS, 0:EMBED], att0T[:, t, :], w_o0[:, t, :], start=t == 0, stop=t == QTILES - 1)
                last.then_inc(S["proj0"], 1)

            def t_int_in(g, p):
                pe.wait_ge(S["int_in"], g + 1)
                after(pe, S["hid1_copied"], g - 1)
                after(pe, S["h2"], g)
                for k in range(2):
                    last = turn(M0[:, :].bitcast(BF16)[0:HALF, k * 128:k * 128 + ROWS],
                                int_in[:, k * HALF:(k + 1) * HALF], ident_b[0:ROWS, 0:ROWS])
                last.then_inc(S["in_turned"], 1)

            def t_gate(g, p):
                pe.wait_ge(S["in_copied"], g + 1)
                after(pe, S["out4_copied"], g - 1)
                for k in range(2):
                    last = pe.matmul(M1[0:ROWS, :], int_inT[:, k, :], w_in[:, k, HIDDEN0:2 * HIDDEN0], start=k == 0, stop=k == 1)
                last.then_inc(S["gate_done"], 1)
                for k in range(2):
                    last = pe.matmul(M0[0:ROWS, :], int_inT[:, k, :], w_in[:, k, 0:HIDDEN0], start=k == 0, stop=k == 1)
                last.then_inc(S["up_done"], 1)

            def t_int_out(g, p):
                pe.wait_ge(S["int_out"], g + 1)
                for k in range(4):
                    last = turn(M1[:, :].bitcast(BF16)[:, k * 128:k * 128 + ROWS],
                                int_out[:, k * 128:(k + 1) * 128], ident_b[0:ROWS, 0:ROWS])
                last.then_inc(S["out_turned"], 1)

            def t_down(g, p):
                pe.wait_ge(S["out_copied"], g + 1)
                for k in range(4):
                    last = pe.matmul(M0[0:ROWS, 0:EMBED], int_outT[:, k, :], w_out[:, k, :], start=k == 0, stop=k == 3)
                last.then_inc(S["down_done"], 1)

            def t_norms2(g, p):
                pe.wait_ge(S["norms2"], g + 1)
                after(pe, S["h3"], g)
                for n in range(2):
                    for k in range(2):
                        last = turn(parts(L0, 4)[0:HALF, 2 * n + k], norms2[:, n, k * HALF:(k + 1) * HALF],
                                    ident[0:ROWS, 0:ROWS])
                last.then_inc(S["norms_turned"], 1)

            def t_lin_in(g, p):
                pe.wait_ge(S["norms_copied"], g + 1)
                for k in range(2):
                    rows = HALF + 1 - k
                    pe.matmul(L0[0:ROWS, 128:128 + EMBED], norms2T[0:rows, 2 + k, :],
                              w_qkv1[0:rows, k, 2 * EMBED:3 * EMBED], start=k == 0, stop=k == 1)
                for k in range(2):
                    last = pe.matmul(L0[:, 0:ROWS], w_g1[:, k, :], norms2T[0:HALF, k, :], start=k == 0, stop=k == 1)
                last.then_inc(S["hid"], 1)
                for j in range(4):
                    for k in range(2):
                        rows = HALF + 1 - k
                        last = pe.matmul(parts(L1, 4)[0:HALF, j], w_qkv1[0:rows, k, j * HALF:(j + 1) * HALF],
                                         norms2T[0:rows, 2 + k, :], start=k == 0, stop=k == 1)
                last.then_inc(S["qk1"], 1)

            def t_params(g, p):
                pe.wait_ge(S["hidT"], g + 1)
                pe.matmul(L0[0:ROWS, 384:384 + HEADS * GATES], hidT[:, :], w_g2[:, :, :].rearrange("p h n -> p (h n)"),
                          start=True, stop=True).then_inc(S["params"], 1)

            def t_lin(quadrants, done_sem):
                def step(g, p):
                    if 0 in quadrants:
                        pe.wait_ge(S["feat_q"], g + 1)
                        pe.wait_ge(S["feat_k"], g + 1)
                        pe.wait_ge(S["tanh_par"], g + 1)
                    else:
                        pe.wait_ge(S["a_masked0"], g + 1)
                    for t in range(2):
                        for odd in range(2):
                            for q in quadrants:
                                last = pe.matmul(parts((L1, L0, L1)[q], 4)[0:ROWS, 2 * t + odd],
                                                 feat_k[32 * q:32 * q + 32, odd, t, :], feat_qk[32 * q:32 * q + 32, t, :],
                                                 start=True, stop=True)
                    last.then_inc(done_sem, 1)
                return step

            def t_num(g, p):
                pe.wait_ge(S["a_masked1"], g + 1)
                pe.wait_ge(S["a_masked2"], g + 1)
                pe.wait_ge(S["a_masked0"], g + 1)
                pe.wait_ge(S["v1"], g + 1)
                for n in range(NUM_TILES):
                    for c in range(128 // SLOT):
                        head = 128 // SLOT * n + c
                        t, q, odd = head // 6, head % 6 // 2, head % 2
                        last = pe.matmul(parts(L0, NUM_TILES)[SLOT * c:SLOT * (c + 1), n], v1[:, head, :],
                                         weightsT[:, 4 * q + 2 * t + odd, :], start=True, stop=True)
                last.then_inc(S["num_done"], 1)

            def t_num_turn(g, p):
                pe.wait_ge(S["num_copied"], g + 1)
                for n in range(NUM_TILES):
                    last = turn(L0[0:ROWS, 128 * n:128 * (n + 1)], numT[:, n, :], ident)
                last.then_inc(S["num"], 1)

            def t_att1(g, p):
                pe.wait_ge(S["att1"], g + 1)
                flat = att1[:, :, :].rearrange("p h d -> p (h d)")
                for k in range(2):
                    last = turn(parts(L1, 2)[0:HALF, k], flat[:, k * HALF:(k + 1) * HALF], ident[0:ROWS, 0:ROWS])
                last.then_inc(S["att1_turned"], 1)

            def t_proj1(g, p):
                pe.wait_ge(S["att1_copied"], g + 1)
                for k in range(2):
                    rows = HALF + 1 - k
                    last = pe.matmul(L0[0:ROWS, 256:256 + EMBED], att1T[0:rows, k, :], w_p1[0:rows, k, :],
                                     start=k == 0, stop=k == 1)
                last.then_inc(S["proj1"], 1)

            def of_stage2(count):
                return min(count, GROUPS) if isinstance(count, int) else count

            def t_norm3(g, p):
                pe.wait_ge(S["norm3"], g + 1)
                after(pe, S["out4_copied"], g)
                pe.wait_ge(S["out_copied"], of_stage2(g + 2))
                for k in range(2):
                    last = turn(parts(M1, 2)[0:HALF, k], norm3[:, k * HALF:(k + 1) * HALF], ident[0:ROWS, 0:ROWS])
                last.then_inc(S["norm3_turned"], 1)

            def t_hid1(g, p):
                pe.wait_ge(S["norm3_copied"], g + 1)
                pe.wait_ge(S["h2"], of_stage2(g + 2))
                for k in range(2):
                    rows = HALF + 1 - k
                    last = pe.matmul(M0[:, 0:ROWS], w1[0:rows, k, :], norm3T[0:rows, k, :], start=k == 0, stop=k == 1)
                last.then_inc(S["hid1"], 1)

            def t_out4(g, p):
                pe.wait_ge(S["hid1_copied"], g + 1)
                pe.matmul(M1[0:ROWS, 0:EMBED], hid1T[:, :], w2o[:, :], start=True, stop=True).then_inc(S["out4"], 1)

            iterations(pe, lambda i, parity, active: in_turn(i, parity, active, [
                (5, t_norm3), (1, t_qk(0)), (4, t_params), (5, t_hid1), (1, t_qk(1)), (3, t_int_in), (5, t_out4),
                (4, t_lin((0, 1), S["a_done01"])), (2, t_probs(0)), (3, t_gate), (2, t_probs(1)), (2, t_probs(2)),
                (4, t_lin((2,), S["a_done2"])), (1, t_qk(2)), (2, t_att0(0)), (4, t_num), (2, t_att0(1)),
                (0, t_patches(1, E1, S["qk_copied1"], S["patches1"])), (4, t_num_turn), (2, t_proj0),
                (0, t_patches(0, E0, S["qk_copied2"], S["patches0"])), (3, t_int_out), (1, t_dots(0)), (0, t_embed),
                (3, t_down), (1, t_dots(1)), (4, t_att1), (0, t_norm0), (4, t_proj1), (0, t_v(0)), (3, t_norms2),
                (0, t_v(1)), (3, t_lin_in),
            ]), setup)


def kernel(**inputs):
    import concourse.bacc as bacc
    from concourse.bass_utils import run_bass_kernel_spmd

    nc = bacc.Bacc("TRN2", target_bir_lowering=False, num_devices=1)
    arrays, handles = {}, {}
    for name, value in inputs.items():
        arrays[name] = np.ascontiguousarray(value)
        handles[name] = nc.dram_tensor(name, arrays[name].shape, F32, kind="ExternalInput").ap()
    arrays["constants"] = constant_table()
    table = nc.dram_tensor("constants", arrays["constants"].shape, F32, kind="ExternalInput").ap()
    out = nc.dram_tensor("out", (IMAGES, TOKENS, EMBED), F32, kind="ExternalOutput").ap()
    build(nc, handles, table, out.rearrange("b t n -> (b t) n"))
    return run_bass_kernel_spmd(nc, [arrays], core_ids=[0]).results[0]["out"]
```
